# Optimizing a Trainium2 kernel written in Bass

```python
import numpy as np
import jax
import jax.numpy as jnp

def _softmax(x, axis=-1):
    return jax.nn.softmax(x, axis=axis)

def _gelu(x):
    return jax.nn.gelu(x, approximate=True)

def _silu(x):
    return jax.nn.silu(x)

def _sigmoid(x):
    return jax.nn.sigmoid(x)

def _layernorm(x, axis=-1, eps=1e-05):
    m = jnp.mean(x, axis=axis, keepdims=True)
    v = jnp.var(x, axis=axis, keepdims=True)
    return (x - m) / jnp.sqrt(v + eps)

def _scatter_add(tgt, idx, src, axis=0):
    return tgt.at[idx].add(src)

def _segment_sum(src, seg, n):
    return jax.ops.segment_sum(src, seg, n)
kernel_name = 'mk_prb_d1_jaxref_r4_28d920'

def setup_inputs(seed: int=0):
    np.random.seed(seed)
    _w = jnp.asarray

    def _L0_attn_setup():
        import math
        import jax, jax.numpy as jnp
        import numpy as np
        B, S, D, H = (2, 512, 256, 16)
        HD = D // H
        LAMBDA_MAX = 0.5
        AMP_EPS = 1e-06

        def _amp_norm(t):
            a = jax.nn.softplus(t)
            return a / jnp.sqrt(jnp.mean(a * a, axis=-1, keepdims=True) + AMP_EPS)
        key = jax.random.key(seed)
        ks = jax.random.split(key, 8)
        x = jax.random.normal(ks[0], (B, S, D), jnp.float32)
        w = lambda k, std: std * jax.random.normal(k, (D, D), jnp.float32)
        return {'x': x, 'Wq': w(ks[1], 0.02), 'Wk': w(ks[2], 0.02), 'Wv': w(ks[3], 0.02), 'Wo': w(ks[4], 0.02), 'Wqp': w(ks[5], 0.005), 'Wkp': w(ks[6], 0.005), 'lambda_raw': jnp.full((H,), float(np.arctanh(0.5)), jnp.float32)}
    _L0_attn_in = _L0_attn_setup()

    def _L0_ffn_setup():
        import jax, jax.numpy as jnp
        import numpy as np
        DIM = 256
        HIDDEN = 768
        SCALE = 1.0 / 127.0

        def _dequant(w_int, dtype):
            return w_int.astype(dtype) * jnp.asarray(SCALE, dtype)
        key = jax.random.key(seed)
        k_x, k_g, k_u, k_d = jax.random.split(key, 4)
        x = jax.random.normal(k_x, (4, 512, DIM), dtype=jnp.float32)
        w_gate = jax.random.randint(k_g, (HIDDEN, DIM), -127, 128, dtype=jnp.int32)
        w_up = jax.random.randint(k_u, (HIDDEN, DIM), -127, 128, dtype=jnp.int32)
        w_down = jax.random.randint(k_d, (DIM, HIDDEN), -127, 128, dtype=jnp.int32)
        return {'x': x, 'w_gate': w_gate, 'w_up': w_up, 'w_down': w_down}
    _L0_ffn_in = _L0_ffn_setup()
    _d = {'L0_attn_x': _L0_attn_in['x'], 'L0_attn_Wq': _L0_attn_in['Wq'], 'L0_attn_Wk': _L0_attn_in['Wk'], 'L0_attn_Wv': _L0_attn_in['Wv'], 'L0_attn_Wo': _L0_attn_in['Wo'], 'L0_attn_Wqp': _L0_attn_in['Wqp'], 'L0_attn_Wkp': _L0_attn_in['Wkp'], 'L0_attn_lambda_raw': _L0_attn_in['lambda_raw'], 'L0_ffn_w_gate': _L0_ffn_in['w_gate'], 'L0_ffn_w_up': _L0_ffn_in['w_up'], 'L0_ffn_w_down': _L0_ffn_in['w_down']}
    _x0 = _d['L0_attn_x']
    _d['L0_attn_x'] = jax.random.normal(jax.random.fold_in(jax.random.key(seed), 1), (8, 512, 256), dtype=_x0.dtype)
    del _x0
    return _d

def reference(L0_attn_x, L0_attn_Wq, L0_attn_Wk, L0_attn_Wv, L0_attn_Wo, L0_attn_Wqp, L0_attn_Wkp, L0_attn_lambda_raw, L0_ffn_w_gate, L0_ffn_w_up, L0_ffn_w_down):

    def _L0_attn_ref(x, Wq, Wk, Wv, Wo, Wqp, Wkp, lambda_raw):
        import math
        import jax, jax.numpy as jnp
        import numpy as np
        B, S, D, H = (2, 512, 256, 16)
        HD = D // H
        LAMBDA_MAX = 0.5
        AMP_EPS = 1e-06

        def _amp_norm(t):
            a = jax.nn.softplus(t)
            return a / jnp.sqrt(jnp.mean(a * a, axis=-1, keepdims=True) + AMP_EPS)
        b, s, d = x.shape
        split = lambda t: t.reshape(b, s, H, HD)
        q = split(x @ Wq)
        k = split(x @ Wk)
        v = split(x @ Wv)
        scale = 1.0 / math.sqrt(HD)
        scores_dot = jnp.einsum('bihd,bjhd->bhij', q, k) * scale
        q_amp = _amp_norm(q)
        k_amp = _amp_norm(k)
        q_phi = math.pi * jnp.tanh(split(x @ Wqp))
        k_phi = math.pi * jnp.tanh(split(x @ Wkp))
        q_cos = q_amp * jnp.cos(q_phi)
        q_sin = q_amp * jnp.sin(q_phi)
        k_cos = k_amp * jnp.cos(k_phi)
        k_sin = k_amp * jnp.sin(k_phi)
        scores_phase = (jnp.einsum('bihd,bjhd->bhij', q_cos, k_cos) + jnp.einsum('bihd,bjhd->bhij', q_sin, k_sin)) * scale
        lam = (LAMBDA_MAX * jnp.tanh(lambda_raw))[None, :, None, None]
        scores = scores_dot + lam * scores_phase
        causal = jnp.tril(jnp.ones((s, s), bool))
        scores = jnp.where(causal[None, None], scores, -jnp.inf)
        attn = jax.nn.softmax(scores, axis=-1)
        out = jnp.einsum('bhij,bjhd->bihd', attn, v).reshape(b, s, d)
        return out @ Wo

    def _L0_ffn_ref(x, w_gate, w_up, w_down):
        import jax, jax.numpy as jnp
        import numpy as np
        DIM = 256
        HIDDEN = 768
        SCALE = 1.0 / 127.0

        def _dequant(w_int, dtype):
            return w_int.astype(dtype) * jnp.asarray(SCALE, dtype)
        wg = _dequant(w_gate, x.dtype)
        wu = _dequant(w_up, x.dtype)
        wd = _dequant(w_down, x.dtype)
        gate = jnp.einsum('bsd,hd->bsh', x, wg)
        up = jnp.einsum('bsd,hd->bsh', x, wu)
        h = jax.nn.silu(gate) * up
        return jnp.einsum('bsh,dh->bsd', h, wd)
    x = L0_attn_x
    xn = _layernorm(x, axis=-1)
    x = x + _L0_attn_ref(xn, L0_attn_Wq, L0_attn_Wk, L0_attn_Wv, L0_attn_Wo, L0_attn_Wqp, L0_attn_Wkp, L0_attn_lambda_raw) + _L0_ffn_ref(xn, L0_ffn_w_gate, L0_ffn_w_up, L0_ffn_w_down)
    return x

_drawn_inputs = setup_inputs


def setup_inputs(seed=0):
    import zlib

    import numpy as np

    out = dict(_drawn_inputs(seed))
    spreads = {'L0_attn_lambda_raw': (0.5493061542510986, 0.6)}
    factors = {'L0_attn_Wq': 64.0,
     'L0_attn_Wk': 64.0,
     'L0_attn_Wv': 64.0,
     'L0_attn_Wo': 64.0,
     'L0_attn_Wqp': 64.0,
     'L0_attn_Wkp': 64.0}
    for name, (base, spread) in spreads.items():
        noise = np.random.default_rng([zlib.crc32(name.encode()), seed]).standard_normal(out[name].shape)
        drawn = base * np.exp(spread * noise) if base else spread * noise
        out[name] = jnp.asarray(drawn.astype(out[name].dtype))
    for name, factor in factors.items():
        out[name] = (out[name] * factor).astype(out[name].dtype)
    return out
```

```python
from contextlib import ExitStack
from math import pi

import concourse.bass as bass
from concourse import mybir

F32 = mybir.dt.float32
F16 = mybir.dt.float16
I32 = mybir.dt.int32
ALU = mybir.AluOpType
ACT = mybir.ActivationFunctionType
AX_X = mybir.AxisListType.X

P = 128
BIG = 60000.0
W_SCALE = 16.0
SHIFT = 16.0
ABS_BITS = 0x7FFFFFFF
H_SCALE = 16.0
EXP_SET = "natural_log_exp_and_others"
TRIG_SET = "silu_and_others"


def phase_attention_and_ffn(nc, x, wq, wk, wv, wo, wqp, wkp, lam_raw, w_gate, w_up, w_down, out):
    B, S, D = x.shape
    HID = w_gate.shape[0]
    H = lam_raw.shape[0]
    HD = D // H
    NT = S // P
    C = D // P
    NH = HID // P
    U = 2
    HU = H // U
    QH = 4
    NF = 3
    R = NF * HD
    TRI = P * NT * (NT + 1) // 2
    FILLS = 10
    NORM_EPS, AMP_EPS = 1e-5, 1e-6
    SCORE = float(HD) ** -0.5
    DEQ = 1.0 / 127.0

    S_FILL = [[(0, 0, 0, 512)], [(0, 1, 0, 384), (0, 3, 384, 128)],
              [(1, 0, 0, 512)], [(1, 1, 0, 384), (1, 3, 384, 128)],
              [(0, 2, 0, 256), (1, 2, 256, 256)]]
    M_FILL = [[(0, 3, 0, 512)], [(0, 2, 0, 384), (0, 0, 384, 128)],
              [(1, 3, 0, 512)], [(1, 2, 0, 384), (1, 0, 384, 128)],
              [(0, 1, 0, 256), (1, 1, 256, 256)]]
    P_PLACE = [0, 512, 1024, 1536, 2048]

    def p_columns(head, kt):
        pair, hp = head // 2, head % 2
        for f, fill in enumerate(S_FILL):
            for (h2, t2, col, _) in fill:
                if (h2, t2) == (hp, kt):
                    return pair * 2 * TRI + P_PLACE[f] + col

    def schedule(front, back):
        at = {}

        def put(pos, *items):
            at.setdefault(pos, []).extend(items)

        if front:
            put(0, ("LN",)), put(2, ("T",))
            for j, o in ((0, 4), (1, 11)):
                put(o, ("QK", j)), put(o + 1, ("AB", j)), put(o + 2, ("EL", j)), put(o + 3, ("AA", j))
                put(o + 5, ("MS", j)), put(o + 6, ("GG", j))
            put(19.5, ("TRIG",), ("PP", 0), ("PP", 1), ("SC", 0), ("CS", 0), ("SC", 1), ("CS", 1), ("HL", 0),
                *[("FG", n) for n in range(NH)], ("EXPS",), ("HL", 1))
            put(32, ("ST", 0, 0)), put(40, ("ST", 0, 1), ("V",))
        if back:
            put(12, ("ST", 1, 0), ("PV", 0)), put(14, ("OT", 0)), put(22, ("ST", 1, 1), ("PV", 1)), put(24, ("OT", 1))
            put(32.5, ("PV", 2)), put(34, ("OT", 2))
            put(39.5, ("PV", 3), ("OT", 3), ("AT",), ("OP",))
        if front:
            put(41, ("DN",))
        steps = []
        for pos in range(42):
            if pos < 40:
                w, q, k = pos // 20, pos % 20 // 10, pos % 10
                if back:
                    steps.append(("S", w, q, k))
                if (back and w == 0) or (front and w == 1):
                    steps.append(("M", 1 - w, q, k))
            steps += at.get(pos, []) + at.get(pos + 0.5, [])
        return steps

    with ExitStack() as ctx:
        def sb(name, shape, dt=F32):
            return ctx.enter_context(nc.sbuf_tensor(name, shape, dt))

        def ps(name, shape):
            return ctx.enter_context(nc.psum_tensor(name, shape, F32))

        def sem(name):
            return ctx.enter_context(nc.semaphore(name))

        ps_s = ps("ps_s", [P, 2, 512])
        ps_m = ps("ps_m", [P, 2, 512])
        ps_o = ps("ps_o", [P, 512])
        ps_t = ps("ps_t", [P, 512])
        ps_w = ps("ps_w", [P, 2, 512])

        stack_q = sb("stack_q", [P, U, HU, S], F16)
        stack_kh = sb("stack_kh", [P, U, HU, S], F16)
        stack_kl = sb("stack_kl", [P, U, HU, S], F16)
        probs = sb("probs", [P, 2, QH * TRI])
        part_hi = sb("part_hi", [P, NF, 2, S], F16)
        part_lo = sb("part_lo", [P, NF, 2, S], F16)
        feat_t = sb("feat_t", [P, U, 2, S])
        feat_w = sb("feat_w", [P, 2, S])
        feat_a = sb("feat_a", [P, U, 2, S])
        feat_s = sb("feat_s", [P, U, 2, S])
        feat_c = sb("feat_c", [P, U, 2, S])
        x_in = sb("x_in", [P, NT, D])
        xn = sb("xn", [P, NT, D])
        x_hi = sb("x_hi", [P, C, S], F16)
        x_lo = sb("x_lo", [P, C, S], F16)
        v_sb = sb("v_sb", [P, NT, H, HD + 1])
        attn = sb("attn", [P, NT, D])
        y_sb = sb("y_sb", [P, NT, D])
        h_hi = sb("h_hi", [P, NH, S], F16)
        h_lo = sb("h_lo", [P, NH, S], F16)
        o_sb = sb("o_sb", [P, S])
        w_qkv = sb("w_qkv", [P, 5, 2, C, D], F16)
        w_o = sb("w_o", [P, 2, C, D], F16)
        w_gu = sb("w_gu", [P, 2, 2, C, HID], F16)
        w_d = sb("w_d", [P, 2, NH, D], F16)
        ident = sb("ident", [P, P])
        big_ident = sb("big_ident", [P, P], F16)
        mask_t = sb("mask_t", [P, P], F16)
        mask_m = sb("mask_m", [P, P], F16)
        same_head = sb("same_head", [P, P])
        lam = sb("lam", [P, U])
        stats = sb("stats", [P, NT, 6])
        mean_var = sb("mean_var", [P, NT, 2])
        rstd = sb("rstd", [P, NT])
        newton = sb("newton", [P, NT])
        neg_max = sb("neg_max", [P, 2, QH, NT])
        shift = sb("shift", [QH * NT, 2, P], F16)
        recip = sb("recip", [P, NT, QH])
        ao_hi = xn[:].rearrange("p a b -> p (a b)").bitcast(F16)[:, 0:C * S].rearrange("p (c s) -> p c s", c=C)
        ao_lo = xn[:].rearrange("p a b -> p (a b)").bitcast(F16)[:, C * S:2 * C * S].rearrange("p (c s) -> p c s", c=C)

        loaded, consts, cleared, converted = sem("loaded"), sem("consts"), sem("cleared"), sem("converted")
        turned, split_done, lam_done = sem("turned"), sem("split_done"), sem("lam_done")

        per = {}

        def step_sem(name, n):
            s = sem(name)
            per[id(s)] = n
            return s

        x_loaded = step_sem("x_loaded", 16)
        ln_stats, ln_aggr, ln_root, ln_newton, ln_done = (step_sem(n, k) for n, k in (
            ("ln_stats", NT), ("ln_aggr", NT), ("ln_root", 2), ("ln_newton", 3), ("ln_done", NT)))
        ln_newton_end = step_sem("ln_newton_end", 1)
        xt_ready, xhi_ready, xlo_ready = (step_sem(n, 1) for n in ("xt_ready", "xhi_ready", "xlo_ready"))
        qk_ready, t_ready, abs_ready, e_ready, l_ready, a_ready, sq_ready = (step_sem(n, 2) for n in (
            "qk_ready", "t_ready", "abs_ready", "e_ready", "l_ready", "a_ready", "sq_ready"))
        ms_ready, msln_ready, r_ready = (step_sem(n, 2) for n in ("ms_ready", "msln_ready", "r_ready"))
        g_ready = step_sem("g_ready", 4)
        pp_ready, th_ready, abst_ready, cos_ready, sin_ready = (step_sem(n, 2) for n in (
            "pp_ready", "th_ready", "abst_ready", "cos_ready", "sin_ready"))
        cs_ready, hi_ready, lo_ready = (step_sem(n, k) for n, k in (("cs_ready", 4), ("hi_ready", 2 * NF), ("lo_ready", 2 * NF)))
        NDMA = NF * 6
        stacked = [step_sem(f"stacked{q}", 16 * NDMA * U) for q in range(2)]
        max_filled = [step_sem(f"max_filled{j}", 2 * FILLS) for j in range(U)]
        max_read = [step_sem(f"max_read{j}", 2 * FILLS) for j in range(U)]
        turned_max = [step_sem(f"turned_max{j}", 2) for j in range(U)]
        shift_ready = [step_sem(f"shift_ready{j}", 2) for j in range(U)]
        shift_stored = [[step_sem(f"shift_stored{j}{q}", 16) for q in range(2)] for j in range(U)]
        v_ready, v_stored = step_sem("v_ready", 1), step_sem("v_stored", 1)
        gate_ready, silu_ready, h_ready, hhi_ready, hlo_ready = (step_sem(n, NH) for n in (
            "gate_ready", "silu_ready", "h_ready", "hhi_ready", "hlo_ready"))
        down_ready, y_ready = step_sem("down_ready", 1), step_sem("y_ready", 1)
        s_filled, exp_done = step_sem("s_filled", 4 * FILLS), step_sem("exp_done", 4 * FILLS)
        pv_done, o_copied, o_turned, o_recip, o_normed = (step_sem(n, 4) for n in (
            "pv_done", "o_copied", "o_turned", "o_recip", "o_normed"))
        at_ready, aohi_ready, aolo_ready, op_ready, res_ready = (step_sem(n, 1) for n in (
            "at_ready", "aohi_ready", "aolo_ready", "op_ready", "res_ready"))
        stored = step_sem("stored", 16)
        gate = sem("gate")

        def now(s, i, c):
            return i * per[id(s)] + c

        def past(s, i, c):
            return i * per[id(s)] + (c - per[id(s)])

        w_released = {"T": (xlo_ready, 1), "QK": (t_ready, 2), "MS": (msln_ready, 2), "PP": (th_ready, 2),
                      "V": (v_stored, 1), "FG": (h_ready, NH), "DN": (y_ready, 1), "AT": (aolo_ready, 1), "OP": (res_ready, 1)}

        block = ctx.enter_context(nc.Block())

        def steps_of(eng, emit):
            emit(0, schedule(True, False), first=True)
            with eng.Fori(1, B) as i:
                emit(i, schedule(True, True))
            emit(B, schedule(False, True))

        raw_w = probs[:, 0, :]
        raw = [raw_w[:, n * C * D:(n + 1) * C * D].rearrange("p (c d) -> p c d", c=C) for n in range(6)]
        off = 6 * C * D
        flat = probs[:].rearrange("p a b -> p (a b)")
        raw_g = [flat[:, off + n * NH * D:off + (n + 1) * NH * D] for n in range(2)]
        raw_d = flat[:, off + 2 * NH * D:off + 3 * NH * D]

        @block.sync
        def _(sp):
            for n, w in enumerate((wq, wk, wqp, wkp, wv, wo)):
                sp.dma_start(raw[n], w.rearrange("(c p) d -> p c d", p=P)).then_inc(loaded, 16)
            for n, w in enumerate((w_gate, w_up)):
                sp.dma_start(raw_g[n].bitcast(I32).rearrange("p (n d) -> p n d", n=NH),
                             w.rearrange("(n p) d -> p n d", p=P)).then_inc(loaded, 16)
            sp.dma_start(raw_d.bitcast(I32).rearrange("p (c n) -> p c n", c=C),
                         w_down.rearrange("(c p) n -> p c n", p=P)).then_inc(loaded, 16)
            for j in range(U):
                for q in range(2):
                    src = bass.AP(lam_raw.tensor, j * HU + q * QH, [[0, HD], [1, QH], [1, 1]])
                    sp.dma_start(lam[64 * q:64 * q + 64, j:j + 1], src).then_inc(loaded, 16)

            def emit(i, steps, first=False):
                front = ("LN",) in steps
                back = ("AT",) in steps

                def stack_dmas(j, q, ahead):
                    rows = slice(64 * q, 64 * q + 64)
                    heads = slice(QH * q, QH * q + QH)
                    for m in range(NF):
                        for part, src in enumerate((part_hi, part_lo)):
                            r = R * part + HD * m
                            sp.dma_start(stack_q[r:r + HD, j, heads, :], src[rows, m, 0, :]).then_inc(stacked[q], 16)
                        for part in range(2):
                            r = R * part + HD * m
                            sp.dma_start(stack_kh[r:r + HD, j, heads, :], part_hi[rows, m, 1, :]).then_inc(stacked[q], 16)
                            sp.dma_start(stack_kl[r:r + HD, j, heads, :], part_lo[rows, m, 1, :]).then_inc(stacked[q], 16)

                for s in steps:
                    if s[0] == "LN":
                        if not first:
                            sp.wait_ge(y_ready, past(y_ready, i, 1))
                            sp.sem_inc(gate, 1)
                        sp.dma_start(x_in[:], x[i].rearrange("(t p) d -> p t d", p=P)).then_inc(x_loaded, 16)
                    elif s[0] == "HL" and s[1] == 0:
                        for q in range(2):
                            sp.wait_ge(hi_ready, now(hi_ready, i, NF))
                            sp.sem_inc(gate, 1)
                            sp.wait_ge(lo_ready, now(lo_ready, i, NF))
                            sp.sem_inc(gate, 1)
                            if back:
                                sp.wait_ge(s_filled, now(s_filled, i, FILLS * (q + 1)))
                                sp.sem_inc(gate, 1)
                            stack_dmas(0, q, 0)
                    elif s == ("S", 1, 1, 0) and front:
                        sp.wait_ge(hi_ready, now(hi_ready, i, 2 * NF))
                        sp.sem_inc(gate, 1)
                        sp.wait_ge(lo_ready, now(lo_ready, i, 2 * NF))
                        sp.sem_inc(gate, 1)
                        sp.wait_ge(s_filled, now(s_filled, i, FILLS * 3))
                        sp.sem_inc(gate, 1)
                        stack_dmas(1, 0, 0)
                    elif s[0] == "DN":
                        if not back:
                            sp.wait_ge(hi_ready, now(hi_ready, i, 2 * NF))
                            sp.sem_inc(gate, 1)
                            sp.wait_ge(lo_ready, now(lo_ready, i, 2 * NF))
                            sp.sem_inc(gate, 1)
                            stack_dmas(1, 0, 0)
                        else:
                            sp.wait_ge(s_filled, now(s_filled, i, FILLS * 4))
                            sp.sem_inc(gate, 1)
                        stack_dmas(1, 1, 0)
                    elif s[0] == "ST":
                        _, j, q = s
                        sp.wait_ge(shift_ready[j], now(shift_ready[j], i, q + 1))
                        sp.sem_inc(gate, 1)
                        sp.dma_start(stack_q[2 * R:2 * R + 1, j, QH * q:QH * q + QH, :],
                                     shift[:, q, :]).then_inc(shift_stored[j][q], 16)
                    elif s[0] == "OP":
                        sp.wait_ge(res_ready, now(res_ready, i, 1))
                        sp.sem_inc(gate, 1)
                        sp.dma_start(out[i - 1].rearrange("(t p) d -> p t d", p=P), attn[:]).then_inc(stored, 16)

            steps_of(sp, emit)
            sp.wait_ge(stored, 16 * (B + 1))

        @block.gpsimd
        def _(pool):
            pool.memset(ident[:], 0.0).then_inc(consts, 1)
            pool.memset(big_ident[:], 0.0).then_inc(consts, 1)
            pool.memset(mask_t[:], 0.0).then_inc(consts, 1)
            pool.memset(mask_m[:], 0.0).then_inc(consts, 1)
            pool.memset(same_head[:], 0.0).then_inc(consts, 1)
            pool.memset(v_sb[:], 1.0).then_inc(consts, 1)
            pool.wait_ge(consts, 6)
            pool.affine_select(out=ident[:], in_=ident[:], compare_op=ALU.not_equal, fill=1.0, base=0,
                               pattern=[[-1, P]], channel_multiplier=1).then_inc(consts, 1)
            pool.affine_select(out=big_ident[:], in_=big_ident[:], compare_op=ALU.not_equal, fill=BIG, base=0,
                               pattern=[[-1, P]], channel_multiplier=1).then_inc(consts, 1)
            pool.affine_select(out=mask_t[:], in_=mask_t[:], compare_op=ALU.is_ge, fill=-BIG, base=0,
                               pattern=[[1, P]], channel_multiplier=-1).then_inc(consts, 1)
            pool.affine_select(out=mask_m[:], in_=mask_m[:], compare_op=ALU.is_ge, fill=-BIG, base=0,
                               pattern=[[-1, P]], channel_multiplier=1).then_inc(consts, 1)
            for e in range(-(HD - 1), HD):
                v = same_head[:].rearrange("p (q c) -> p q c", q=2)
                pool.affine_select(out=v, in_=v, compare_op=ALU.not_equal, fill=1.0, base=-QH * e,
                                   pattern=[[-64, 2], [-1, 64]], channel_multiplier=1).then_inc(consts, 1)
                pool.wait_ge(consts, 11 + e + HD - 1)
            pool.memset(same_head[0:64, 64:128], 0.0).then_inc(consts, 1)
            pool.memset(same_head[64:128, 0:64], 0.0).then_inc(consts, 1)
            for s, k in ((s_filled, 1), (exp_done, 1), (pv_done, 1), (o_copied, 1), (o_turned, 1), (o_recip, 1),
                         (o_normed, 1), (at_ready, 1), (aohi_ready, 1), (aolo_ready, 1), (op_ready, 1),
                         (res_ready, 1), (stored, 1), (max_filled[1], 1), (max_read[1], 1), (turned_max[1], 1),
                         (shift_ready[1], 1), (shift_stored[1][0], 1), (shift_stored[1][1], 1)):
                pool.sem_inc(s, per[id(s)])

            def emit(i, steps, first=False):
                for s in steps:
                    if s[0] == "AA":
                        j = s[1]
                        pool.wait_ge(a_ready, now(a_ready, i, j + 1))
                        pool.tensor_tensor(feat_w[:], feat_a[:, j], feat_a[:, j], ALU.mult).then_inc(sq_ready, 1)
                    elif s[0] == "HL":
                        j = s[1]
                        if j == 0:
                            for q in range(2):
                                if not first:
                                    pool.wait_ge(stacked[q], past(stacked[q], i, 32 * NDMA))
                                    pool.sem_inc(gate, 1)
                        else:
                            for q in range(2):
                                pool.wait_ge(stacked[q], now(stacked[q], i, 16 * NDMA))
                                pool.sem_inc(gate, 1)
                        pool.wait_ge(t_ready, now(t_ready, i, j + 1))
                        pool.sem_inc(gate, 1)
                        for m, src in enumerate((feat_t, feat_c, feat_s)):
                            if m:
                                pool.wait_ge(cs_ready, now(cs_ready, i, 2 * j + m))
                                pool.sem_inc(gate, 1)
                            pool.tensor_scalar(part_hi[:, m], src[:, j], 1.0, 0.0, ALU.mult, ALU.add).then_inc(hi_ready, 1)

            steps_of(pool, emit)

        @block.scalar
        def _(act):
            act.preload_act_table_set(TRIG_SET)
            act.wait_ge(loaded, 16 * 13)
            act.activation(lam[:], lam[:], ACT.Tanh).then_inc(lam_done, 1)
            act.preload_act_table_set(EXP_SET)

            def emit(i, steps, first=False):
                for s in steps:
                    k = s[0]
                    if k == "LN":
                        act.wait_ge(ln_aggr, now(ln_aggr, i, NT))
                        act.activation(rstd[:], mean_var[:, :, 1], ACT.Ln, bias=NORM_EPS).then_inc(ln_root, 1)
                        act.wait_ge(ln_root, now(ln_root, i, 1))
                        act.activation(rstd[:], rstd[:], ACT.Exp, scale=-0.5).then_inc(ln_root, 1)
                    elif k == "T":
                        act.wait_ge(xt_ready, now(xt_ready, i, 1))
                        act.activation(x_hi[:], ps_w[:], ACT.Copy).then_inc(xhi_ready, 1)
                    elif k == "QK":
                        j = s[1]
                        act.wait_ge(qk_ready, now(qk_ready, i, j + 1))
                        if not first:
                            act.wait_ge(lo_ready, past(lo_ready, i, NF * j + 1))
                        act.activation(feat_t[:, j], ps_w[:], ACT.Copy, scale=1.0 / W_SCALE).then_inc(t_ready, 1)
                    elif k == "EL":
                        j = s[1]
                        act.wait_ge(abs_ready, now(abs_ready, i, j + 1))
                        act.activation(feat_w[:], feat_w[:], ACT.Exp, scale=-1.0).then_inc(e_ready, 1)
                        act.wait_ge(e_ready, now(e_ready, i, j + 1))
                        act.activation(feat_w[:], feat_w[:], ACT.Ln, bias=1.0).then_inc(l_ready, 1)
                    elif k == "MS":
                        j = s[1]
                        act.wait_ge(ms_ready, now(ms_ready, i, j + 1))
                        act.activation(feat_w[:], ps_w[:], ACT.Ln, scale=1.0 / HD, bias=AMP_EPS).then_inc(msln_ready, 1)
                        act.wait_ge(msln_ready, now(msln_ready, i, j + 1))
                        act.activation(feat_w[:], feat_w[:], ACT.Exp, scale=-0.5).then_inc(r_ready, 1)
                    elif k == "TRIG":
                        act.preload_act_table_set(TRIG_SET)
                    elif k == "EXPS":
                        act.preload_act_table_set(EXP_SET)
                    elif k == "PP":
                        j = s[1]
                        act.wait_ge(pp_ready, now(pp_ready, i, j + 1))
                        if not first:
                            act.wait_ge(lo_ready, past(lo_ready, i, NF * (j + 1)))
                        act.activation(feat_s[:, j], ps_w[:], ACT.Tanh, scale=1.0 / W_SCALE).then_inc(th_ready, 1)
                    elif k == "SC":
                        j = s[1]
                        act.wait_ge(abst_ready, now(abst_ready, i, j + 1))
                        act.activation(feat_c[:, j], feat_c[:, j], ACT.Sin, scale=-pi, bias=pi / 2).then_inc(cos_ready, 1)
                        act.activation(feat_s[:, j], feat_s[:, j], ACT.Sin, scale=pi).then_inc(sin_ready, 1)
                    elif k == "FG":
                        n = s[1]
                        act.wait_ge(gate_ready, now(gate_ready, i, n + 1))
                        if n >= 2:
                            act.wait_ge(hlo_ready, now(hlo_ready, i, n - 1))
                        else:
                            act.wait_ge(g_ready, now(g_ready, i, 4))
                        act.activation(feat_w[:, n % 2], ps_w[:, 0], ACT.Silu, scale=DEQ).then_inc(silu_ready, 1)
                    elif k == "S":
                        _, w, q, f = s
                        n = (2 * w + q) * FILLS + f
                        act.wait_ge(s_filled, now(s_filled, i, n + 1))
                        if f == 0:
                            act.wait_ge(pv_done, now(pv_done, i, 2 * w + q - 1))
                        c0 = (f // 5) * 2 * TRI + P_PLACE[f % 5]
                        act.activation(probs[:, q, c0:c0 + 512], ps_s[:, f % 2], ACT.Exp, scale=SCORE).then_inc(exp_done, 1)
                    elif k == "OT":
                        q = s[1]
                        act.wait_ge(pv_done, now(pv_done, i, q + 1))
                        act.wait_ge(o_turned, now(o_turned, i, q))
                        act.activation(o_sb[:], ps_o[:], ACT.Copy).then_inc(o_copied, 1)
                    elif k == "AT":
                        act.wait_ge(at_ready, now(at_ready, i, 1))
                        act.activation(ao_hi, ps_w[:], ACT.Copy).then_inc(aohi_ready, 1)

            steps_of(act, emit)

        @block.vector
        def _(dve):
            dve.wait_ge(loaded, 16 * 13)
            dve.memset(ps_o[:], 0.0).then_inc(cleared, 1)
            dve.memset(stack_kh[2 * R:2 * R + 1, :, :, :], SHIFT).then_inc(cleared, 1)
            done = 0

            def two(hi, lo, src, scale=1.0):
                nonlocal done
                dve.tensor_scalar(hi, src, scale, None, ALU.mult).then_inc(split_done, 1)
                dve.wait_ge(split_done, done + 1)
                dve.scalar_tensor_tensor(lo, src, scale, hi, ALU.mult, ALU.subtract).then_inc(split_done, 1)
                done += 2

            for n in range(4):
                for c in range(C):
                    for part in range(2 * U):
                        cols = slice(part * 64, part * 64 + 64)
                        view = raw[n][:, c, cols].rearrange("p (h d) -> p d h", d=HD)
                        hi, lo = (w_qkv[:, n, z, c, cols].rearrange("p (d h) -> p d h", h=QH) for z in range(2))
                        two(hi, lo, view, W_SCALE)
            two(w_qkv[:, 4, 0], w_qkv[:, 4, 1], raw[4], W_SCALE)
            two(w_o[:, 0], w_o[:, 1], raw[5], W_SCALE)
            for w in (*raw_g, raw_d):
                dve.tensor_copy(w, w.bitcast(I32)).then_inc(converted, 1)
            for g in range(2):
                for c in range(C):
                    for half in range(2):
                        k = (g * C + c) * 2 + half
                        dve.wait_ge(turned, k + 1)
                        cols = slice(half * 384, half * 384 + 384)
                        two(w_gu[:, g, 0, c, cols], w_gu[:, g, 1, c, cols], ps_w[:, half, 0:384])
            for n in range(NH):
                dve.wait_ge(turned, 8 + n + 1)
                two(w_d[:, 0, n], w_d[:, 1, n], ps_w[:, n % 2, 0:D])
            dve.wait_ge(lam_done, 1)
            dve.tensor_scalar(lam[:], lam[:], 0.5, None, ALU.mult).then_inc(lam_done, 1)

            def emit(i, steps, first=False):
                for s in steps:
                    k = s[0]
                    if k == "LN":
                        dve.wait_ge(x_loaded, now(x_loaded, i, 16))
                        for t in range(NT):
                            dve.bn_stats(stats[:, t], x_in[:, t]).then_inc(ln_stats, 1)
                        for t in range(NT):
                            dve.wait_ge(ln_stats, now(ln_stats, i, t + 1))
                            dve.sem_inc(gate, 1)
                            dve.bn_aggr(mean_var[:, t], stats[:, t]).then_inc(ln_aggr, 1)
                        dve.wait_ge(ln_root, now(ln_root, i, 2))
                        dve.tensor_tensor(newton[:], rstd[:], rstd[:], ALU.mult).then_inc(ln_newton, 1)
                        dve.wait_ge(ln_aggr, now(ln_aggr, i, NT))
                        dve.wait_ge(ln_newton, now(ln_newton, i, 1))
                        dve.scalar_tensor_tensor(newton[:], mean_var[:, :, 1], NORM_EPS, newton[:], ALU.add, ALU.mult).then_inc(ln_newton, 1)
                        dve.wait_ge(ln_newton, now(ln_newton, i, 2))
                        dve.tensor_scalar(newton[:], newton[:], -0.5, 1.5, ALU.mult, ALU.add).then_inc(ln_newton, 1)
                        dve.wait_ge(ln_newton, now(ln_newton, i, 3))
                        dve.tensor_tensor(rstd[:], rstd[:], newton[:], ALU.mult).then_inc(ln_newton_end, 1)
                        dve.wait_ge(ln_newton_end, now(ln_newton_end, i, 1))
                        if not first:
                            dve.wait_ge(op_ready, past(op_ready, i, 1))
                        for t in range(NT):
                            dve.tensor_scalar(xn[:, t], x_in[:, t], mean_var[:, t, 0:1], rstd[:, t:t + 1],
                                              ALU.subtract, ALU.mult).then_inc(ln_done, 1)
                    elif k == "T":
                        dve.wait_ge(xhi_ready, now(xhi_ready, i, 1))
                        dve.tensor_tensor(x_lo[:], ps_w[:], x_hi[:], ALU.subtract).then_inc(xlo_ready, 1)
                    elif k == "AB":
                        j = s[1]
                        dve.wait_ge(t_ready, now(t_ready, i, j + 1))
                        if j:
                            dve.wait_ge(g_ready, now(g_ready, i, 2))
                        else:
                            if not first:
                                dve.wait_ge(hlo_ready, past(hlo_ready, i, NH))
                        dve.tensor_scalar(feat_w[:].bitcast(I32), feat_t[:, j].bitcast(I32), ABS_BITS, None, ALU.bitwise_and).then_inc(abs_ready, 1)
                    elif k == "AA":
                        j = s[1]
                        dve.wait_ge(l_ready, now(l_ready, i, j + 1))
                        if not first:
                            dve.wait_ge(cs_ready, past(cs_ready, i, 2 * j + 2))
                        dve.scalar_tensor_tensor(feat_a[:, j], feat_t[:, j], 0.0, feat_w[:], ALU.max, ALU.add).then_inc(a_ready, 1)
                    elif k == "GG":
                        j = s[1]
                        dve.wait_ge(r_ready, now(r_ready, i, j + 1))
                        dve.wait_ge(sq_ready, now(sq_ready, i, j + 1))
                        dve.tensor_tensor(feat_a[:, j, 0], feat_a[:, j, 0], feat_w[:, 0], ALU.mult).then_inc(g_ready, 1)
                        dve.scalar_tensor_tensor(feat_a[:, j, 1], feat_a[:, j, 1], lam[:, j:j + 1], feat_w[:, 1],
                                                 ALU.mult, ALU.mult).then_inc(g_ready, 1)
                    elif k == "PP":
                        j = s[1]
                        dve.wait_ge(th_ready, now(th_ready, i, j + 1))
                        if not first:
                            dve.wait_ge(lo_ready, past(lo_ready, i, NF * j + 2))
                        dve.tensor_scalar(feat_c[:, j].bitcast(I32), feat_s[:, j].bitcast(I32), ABS_BITS, None, ALU.bitwise_and).then_inc(abst_ready, 1)
                    elif k == "CS":
                        j = s[1]
                        dve.wait_ge(g_ready, now(g_ready, i, 2 * j + 2))
                        dve.wait_ge(cos_ready, now(cos_ready, i, j + 1))
                        dve.tensor_tensor(feat_c[:, j], feat_c[:, j], feat_a[:, j], ALU.mult).then_inc(cs_ready, 1)
                        dve.wait_ge(sin_ready, now(sin_ready, i, j + 1))
                        dve.tensor_tensor(feat_s[:, j], feat_s[:, j], feat_a[:, j], ALU.mult).then_inc(cs_ready, 1)
                    elif k == "HL":
                        j = s[1]
                        for m, src in enumerate((feat_t, feat_c, feat_s)):
                            dve.wait_ge(hi_ready, now(hi_ready, i, NF * j + m + 1))
                            if m:
                                dve.wait_ge(cs_ready, now(cs_ready, i, 2 * j + m))
                            dve.tensor_tensor(part_lo[:, m], src[:, j], part_hi[:, m], ALU.subtract).then_inc(lo_ready, 1)
                    elif k == "M":
                        _, j, q, f = s
                        n = q * FILLS + f
                        dve.wait_ge(max_filled[j], now(max_filled[j], i, n + 1))
                        if f == 0:
                            if j == 0:
                                dve.wait_ge(turned_max[1], now(turned_max[1], i, q + 1))
                            else:
                                if not first:
                                    dve.wait_ge(turned_max[0], past(turned_max[0], i, q + 1))
                        pair = 2 * (f // 5)
                        fill = M_FILL[f % 5]
                        if f % 5 == 4:
                            dve.tensor_reduce(neg_max[:, q, pair:pair + 2, 1], ps_m[:, f % 2].rearrange("p (h c) -> p h c", h=2),
                                              AX_X, ALU.max, negate=True).then_inc(max_read[j], 1)
                        else:
                            for z, (h2, qt, col, width) in enumerate(fill):
                                ins = dve.tensor_reduce(neg_max[:, q, pair + h2, qt:qt + 1], ps_m[:, f % 2, col:col + width],
                                                        AX_X, ALU.max, negate=True)
                                if z == len(fill) - 1:
                                    ins.then_inc(max_read[j], 1)
                    elif k == "ST":
                        _, j, q = s
                        dve.wait_ge(turned_max[j], now(turned_max[j], i, q + 1))
                        if j == 0:
                            dve.wait_ge(shift_stored[1][q], now(shift_stored[1][q], i, 16))
                        else:
                            if not first:
                                dve.wait_ge(shift_stored[0][q], past(shift_stored[0][q], i, 16))
                        dve.tensor_scalar(shift[:, q], ps_t[0:QH * NT, 0:P], 1.0 / SHIFT, None, ALU.mult).then_inc(shift_ready[j], 1)
                    elif k == "OT":
                        q = s[1]
                        dve.wait_ge(o_turned, now(o_turned, i, q + 1))
                        dve.wait_ge(o_normed, now(o_normed, i, q))
                        v = ps_t[:].rearrange("p (t c e) -> p t c e", t=NT, c=QH)
                        dve.reciprocal(recip[:], v[:, :, :, HD]).then_inc(o_recip, 1)
                        dve.wait_ge(o_recip, now(o_recip, i, q + 1))
                        if q == 0:
                            if not first:
                                dve.wait_ge(stored, past(stored, i, 16))
                        o = attn[:, :, QH * HD * q:QH * HD * (q + 1)].rearrange("p t (c d) -> p t c d", c=QH)
                        r = recip[:].unsqueeze(3).to_broadcast([P, NT, QH, HD])
                        dve.tensor_tensor(o, v[:, :, :, 0:HD], r, ALU.mult).then_inc(o_normed, 1)
                    elif k == "AT":
                        dve.wait_ge(aohi_ready, now(aohi_ready, i, 1))
                        dve.tensor_tensor(ao_lo, ps_w[:], ao_hi, ALU.subtract).then_inc(aolo_ready, 1)
                    elif k == "OP":
                        dve.wait_ge(op_ready, now(op_ready, i, 1))
                        if not first:
                            dve.wait_ge(y_ready, past(y_ready, i, 1))
                        dve.scalar_tensor_tensor(attn[:], ps_w[:].rearrange("p a (b d) -> p (a b) d", d=D), 1.0 / W_SCALE, y_sb[:],
                                                 ALU.mult, ALU.add).then_inc(res_ready, 1)
                    elif k == "V":
                        dve.wait_ge(v_ready, now(v_ready, i, 1))
                        dve.wait_ge(pv_done, now(pv_done, i, 4))
                        dve.tensor_scalar(v_sb[:, :, :, 0:HD], ps_w[:].rearrange("p a (b h d) -> p (a b) h d", b=2, d=HD),
                                          1.0 / W_SCALE, None, ALU.mult).then_inc(v_stored, 1)
                    elif k == "FG":
                        n = s[1]
                        dve.wait_ge(silu_ready, now(silu_ready, i, n + 1))
                        dve.scalar_tensor_tensor(feat_w[:, n % 2], ps_w[:, 1], DEQ / H_SCALE, feat_w[:, n % 2], ALU.mult, ALU.mult).then_inc(h_ready, 1)
                        dve.wait_ge(h_ready, now(h_ready, i, n + 1))
                        if n == 0:
                            if not first:
                                dve.wait_ge(down_ready, past(down_ready, i, 1))
                        dve.tensor_copy(h_hi[:, n], feat_w[:, n % 2]).then_inc(hhi_ready, 1)
                        dve.wait_ge(hhi_ready, now(hhi_ready, i, n + 1))
                        dve.tensor_tensor(h_lo[:, n], feat_w[:, n % 2], h_hi[:, n], ALU.subtract).then_inc(hlo_ready, 1)
                    elif k == "DN":
                        dve.wait_ge(down_ready, now(down_ready, i, 1))
                        dve.wait_ge(res_ready, now(res_ready, i, 1))
                        dve.scalar_tensor_tensor(y_sb[:], ps_w[:].rearrange("p a (b d) -> p (a b) d", d=D), DEQ * H_SCALE, x_in[:],
                                                 ALU.mult, ALU.add).then_inc(y_ready, 1)

            steps_of(dve, emit)

        @block.tensor
        def _(pe):
            pe.wait_ge(consts, 6 + 4 + 2 * HD - 1 + 2)
            pe.wait_ge(cleared, 2)
            k = 0
            for g in range(2):
                pe.wait_ge(converted, g + 1)
                for c in range(C):
                    for half in range(2):
                        if k >= 2:
                            pe.wait_ge(split_done, 2 * (4 * C * 2 * U + 2) + 2 * (k - 1))
                        for n in range(3):
                            m = half * 3 + n
                            ins = pe.transpose(ps_w[:, half, n * P:(n + 1) * P], raw_g[g][:, m * D + c * P:m * D + c * P + P], ident[:])
                        ins.then_inc(turned, 1)
                        k += 1
            pe.wait_ge(converted, 3)
            for n in range(NH):
                pe.wait_ge(split_done, 2 * (4 * C * 2 * U + 2) + 2 * (k - 1))
                for c in range(C):
                    ins = pe.transpose(ps_w[:, n % 2, c * P:(c + 1) * P], raw_d[:, c * HID + n * P:c * HID + n * P + P], ident[:])
                ins.then_inc(turned, 1)
                k += 1
            pe.wait_ge(split_done, 2 * (4 * C * 2 * U + 2) + 2 * k)

            HI, LO = 0, 1
            PRODUCTS = ((HI, HI), (LO, HI), (HI, LO))
            xp, hp, aop = (x_hi, x_lo), (h_hi, h_lo), (ao_hi, ao_lo)

            def emit(i, steps, first=False):
                back = ("AT",) in steps
                users = [s for s in steps if s[0] in w_released]

                def take_w(s):
                    at = users.index(s)
                    if at:
                        before = users[at - 1]
                        r, last = w_released[before[0]]
                        pe.wait_ge(r, now(r, i, before[1] + 1 if len(before) > 1 else last))
                    else:
                        if not first:
                            pe.wait_ge(y_ready, past(y_ready, i, 1))

                def project(n, j, qk):
                    k = 0
                    for c in range(C):
                        for wx, xx in PRODUCTS:
                            ins = pe.matmul(ps_w[:, qk], w_qkv[:, n, wx, c, j * P:(j + 1) * P], xp[xx][:, c],
                                            start=(k == 0), stop=(k == 3 * C - 1))
                            k += 1
                    return ins

                def tokens_major(left, right, chunks):
                    for t in range(NT):
                        k = 0
                        for c in range(chunks):
                            for lx, rx in PRODUCTS:
                                ins = pe.matmul(ps_w[:, t // 2, (t % 2) * D:(t % 2 + 1) * D], left[lx][:, c, t * P:(t + 1) * P],
                                                right(rx, c), start=(k == 0), stop=(k == 3 * chunks - 1))
                                k += 1
                    return ins

                for s in steps:
                    k = s[0]
                    if k in w_released:
                        take_w(s)
                    if k == "T":
                        pe.wait_ge(ln_done, now(ln_done, i, NT))
                        for c in range(C):
                            for t in range(NT):
                                ins = pe.transpose(ps_w[:, c, t * P:(t + 1) * P], xn[:, t, c * P:(c + 1) * P], ident[:])
                        ins.then_inc(xt_ready, 1)
                    elif k == "QK":
                        j = s[1]
                        pe.wait_ge(xlo_ready, now(xlo_ready, i, 1))
                        project(0, j, 0)
                        project(1, j, 1).then_inc(qk_ready, 1)
                    elif k == "PP":
                        j = s[1]
                        project(2, j, 0)
                        project(3, j, 1).then_inc(pp_ready, 1)
                    elif k == "MS":
                        j = s[1]
                        pe.wait_ge(sq_ready, now(sq_ready, i, j + 1))
                        for z in range(2):
                            ins = pe.matmul(ps_w[:, z], same_head[:], feat_w[:, z], start=True, stop=True)
                        ins.then_inc(ms_ready, 1)
                    elif k == "V":
                        tokens_major(xp, lambda r, c: w_qkv[:, 4, r, c], C).then_inc(v_ready, 1)
                    elif k == "FG":
                        n = s[1]
                        for g in range(2):
                            k2 = 0
                            for c in range(C):
                                for wx, xx in PRODUCTS:
                                    ins = pe.matmul(ps_w[:, g], w_gu[:, g, wx, c, n * P:(n + 1) * P], xp[xx][:, c],
                                                    start=(k2 == 0), stop=(k2 == 3 * C - 1))
                                    k2 += 1
                        ins.then_inc(gate_ready, 1)
                    elif k == "DN":
                        pe.wait_ge(hlo_ready, now(hlo_ready, i, NH))
                        tokens_major(hp, lambda r, c: w_d[:, r, c], NH).then_inc(down_ready, 1)
                    elif k == "AT":
                        pe.wait_ge(o_normed, now(o_normed, i, 4))
                        for c in range(C):
                            for t in range(NT):
                                ins = pe.transpose(ps_w[:, c, t * P:(t + 1) * P], attn[:, t, c * P:(c + 1) * P], ident[:])
                        ins.then_inc(at_ready, 1)
                    elif k == "OP":
                        pe.wait_ge(aolo_ready, now(aolo_ready, i, 1))
                        tokens_major(aop, lambda r, c: w_o[:, r, c], C).then_inc(op_ready, 1)
                    elif k == "M":
                        _, j, q, f = s
                        n = q * FILLS + f
                        if f == 0:
                            if j == 0:
                                pe.wait_ge(stacked[q], now(stacked[q], i, 16 * NDMA))
                            else:
                                if not first:
                                    pe.wait_ge(stacked[q], past(stacked[q], i, 32 * NDMA))
                        if n >= 2:
                            pe.wait_ge(max_read[j], now(max_read[j], i, n - 1))
                        elif j == 0:
                            pe.wait_ge(max_read[1], now(max_read[1], i, 2 * FILLS - 1 + n))
                        else:
                            if not first:
                                pe.wait_ge(max_read[0], past(max_read[0], i, 2 * FILLS - 1 + n))
                        for h2, qt, col, width in M_FILL[f % 5]:
                            head = QH * q + 2 * (f // 5) + h2
                            o = ps_m[:, f % 2, col:col + width]
                            pe.matmul(o, stack_q[0:2 * R, j, head, qt * P:(qt + 1) * P], stack_kh[0:2 * R, j, head, 0:width],
                                      start=True, stop=False)
                            ins = pe.matmul(ps_m[:, f % 2, col + width - P:col + width], big_ident[:], mask_m[:], start=False, stop=True)
                        ins.then_inc(max_filled[j], 1)
                    elif k == "ST":
                        _, j, q = s
                        pe.wait_ge(max_read[j], now(max_read[j], i, FILLS * (q + 1)))
                        take_t(i, s, steps, first)
                        pe.transpose(ps_t[0:QH * NT, 0:P], neg_max[:, q].rearrange("p h t -> p (h t)"), ident[:]).then_inc(turned_max[j], 1)
                    elif k == "S":
                        _, w, q, f = s
                        n = (2 * w + q) * FILLS + f
                        if f == 0:
                            if w == 0:
                                if not first:
                                    pe.wait_ge(shift_stored[0][q], past(shift_stored[0][q], i, 16))
                            else:
                                pe.wait_ge(shift_stored[1][q], now(shift_stored[1][q], i, 16))
                        if n >= 2:
                            pe.wait_ge(exp_done, now(exp_done, i, n - 1))
                        else:
                            if not first:
                                pe.wait_ge(exp_done, past(exp_done, i, 4 * FILLS - 1 + n))
                        for h2, kt, col, width in S_FILL[f % 5]:
                            head = QH * q + 2 * (f // 5) + h2
                            o = ps_s[:, f % 2, col:col + width]
                            keys, queries = slice(kt * P, (kt + 1) * P), slice(kt * P, S)
                            pe.matmul(o, stack_kh[0:2 * R + 1, w, head, keys], stack_q[0:2 * R + 1, w, head, queries], start=True, stop=False)
                            pe.matmul(o, stack_kl[0:2 * R, w, head, keys], stack_q[0:2 * R, w, head, queries], start=False, stop=False)
                            ins = pe.matmul(ps_s[:, f % 2, col:col + P], big_ident[:], mask_t[:], start=False, stop=True)
                        ins.then_inc(s_filled, 1)
                    elif k == "PV":
                        qd = s[1]
                        pe.wait_ge(exp_done, now(exp_done, i, FILLS * (qd + 1)))
                        pe.wait_ge(o_copied, now(o_copied, i, qd))
                        if qd == 0:
                            if not first:
                                pe.wait_ge(v_stored, past(v_stored, i, 1))
                        for kt in range(NT):
                            for c in range(QH):
                                c0 = p_columns(c, kt)
                                ins = pe.matmul(ps_o[32 * c:32 * c + HD + 1, kt * P:S], v_sb[:, kt, QH * qd + c, :],
                                                probs[:, qd % 2, c0:c0 + S - kt * P], start=(kt == 0), stop=(kt == NT - 1))
                        ins.then_inc(pv_done, 1)
                    elif k == "OT":
                        q = s[1]
                        pe.wait_ge(o_copied, now(o_copied, i, q + 1))
                        take_t(i, s, steps, first)
                        for t in range(NT):
                            ins = pe.transpose(ps_t[:, t * P:(t + 1) * P], o_sb[:, t * P:(t + 1) * P], ident[:])
                        ins.then_inc(o_turned, 1)

            def take_t(i, s, steps, first):
                users = [u for u in steps if u[0] in ("ST", "OT")]
                at = users.index(s)
                if at:
                    u = users[at - 1]
                    if u[0] == "ST":
                        pe.wait_ge(shift_ready[u[1]], now(shift_ready[u[1]], i, u[2] + 1))
                    else:
                        pe.wait_ge(o_normed, now(o_normed, i, u[1] + 1))
                else:
                    if not first:
                        pe.wait_ge(shift_ready[0], past(shift_ready[0], i, 2))
                    if not first:
                        pe.wait_ge(o_normed, past(o_normed, i, 4))

            steps_of(pe, emit)


_INS = ['L0_attn_x', 'L0_attn_Wq', 'L0_attn_Wk', 'L0_attn_Wv', 'L0_attn_Wo', 'L0_attn_Wqp', 'L0_attn_Wkp',
        'L0_attn_lambda_raw', 'L0_ffn_w_gate', 'L0_ffn_w_up', 'L0_ffn_w_down']


def kernel(**inputs):
    import numpy as _np
    import concourse.bacc as _bacc
    from concourse import mybir as _mybir
    from concourse.bass_utils import run_bass_kernel_spmd as _run

    nc = _bacc.Bacc("TRN2", target_bir_lowering=False, num_devices=1)
    arrays, args = {}, []
    for name in _INS:
        a = _np.ascontiguousarray(inputs[name])
        arrays[f"in_{name}"] = a
        args.append(nc.dram_tensor(f"in_{name}", a.shape, _mybir.dt.from_np(a.dtype), kind="ExternalInput").ap())
    shape = inputs['L0_attn_x'].shape
    out = nc.dram_tensor("out_0", shape, _mybir.dt.float32, kind="ExternalOutput").ap()
    phase_attention_and_ffn(nc, *args, out)
    r = _run(nc, [arrays], core_ids=[0])
    return r.results[0]["out_0"]
```

```python
from contextlib import ExitStack
from math import pi

import concourse.bass as bass
from concourse import mybir

F32 = mybir.dt.float32
F16 = mybir.dt.float16
I32 = mybir.dt.int32
ALU = mybir.AluOpType
ACT = mybir.ActivationFunctionType
AX_X = mybir.AxisListType.X

P = 128
BIG = 60000.0
W_SCALE = 16.0
SHIFT = 16.0
ABS_BITS = 0x7FFFFFFF
H_SCALE = 16.0
EXP_SET = "natural_log_exp_and_others"
TRIG_SET = "silu_and_others"


def phase_attention_and_ffn(nc, x, wq, wk, wv, wo, wqp, wkp, lam_raw, w_gate, w_up, w_down, out):
    B, S, D = x.shape
    HID = w_gate.shape[0]
    H = lam_raw.shape[0]
    HD = D // H
    NT = S // P
    C = D // P
    NH = HID // P
    U = 2
    HU = H // U
    QH = 4
    NF = 3
    R = NF * HD
    TRI = P * NT * (NT + 1) // 2
    FILLS = 10
    NORM_EPS, AMP_EPS = 1e-5, 1e-6
    SCORE = float(HD) ** -0.5
    DEQ = 1.0 / 127.0

    S_FILL = [[(0, 0, 0, 512)], [(0, 1, 0, 384), (0, 3, 384, 128)],
              [(1, 0, 0, 512)], [(1, 1, 0, 384), (1, 3, 384, 128)],
              [(0, 2, 0, 256), (1, 2, 256, 256)]]
    M_FILL = [[(0, 3, 0, 512)], [(0, 2, 0, 384), (0, 0, 384, 128)],
              [(1, 3, 0, 512)], [(1, 2, 0, 384), (1, 0, 384, 128)],
              [(0, 1, 0, 256), (1, 1, 256, 256)]]
    P_PLACE = [0, 512, 1024, 1536, 2048]

    def p_columns(head, kt):
        pair, hp = head // 2, head % 2
        for f, fill in enumerate(S_FILL):
            for (h2, t2, col, _) in fill:
                if (h2, t2) == (hp, kt):
                    return pair * 2 * TRI + P_PLACE[f] + col

    def schedule(front, back):
        seq = []
        f = seq.append if front else (lambda s: None)
        b = seq.append if back else (lambda s: None)
        f(("LN",))
        for k in range(FILLS):
            b(("S", 0, 0, k)), b(("M", 1, 0, k))
        f(("T",)), b(("PV", 0)), f(("QK", 0)), b(("ST", 1, 0)), b(("OT", 0)), f(("QK", 1)), f(("TRIG",)), f(("PP", 0)), f(("PP", 1))
        f(("SC", 0)), f(("FG", 0)), f(("SC", 1))
        for n in range(1, NH):
            f(("FG", n))
        f(("EXPS",)), f(("AB", 0))
        after = {0: [("EL", 0)], 2: [("AA", 0), ("SQ", 0)], 4: [("MS", 0)], 5: [("RR", 0)], 6: [("GG", 0), ("AB", 1)],
                 7: [("EL", 1), ("CS", 0)], 9: [("HL", 0), ("AA", 1), ("SQ", 1)]}
        for k in range(FILLS):
            b(("S", 0, 1, k)), b(("M", 1, 1, k))
            for s in after.get(k, []):
                f(s)
        f(("DM", 0))
        behind = {0: [("ST", 1, 1)], 2: [("PV", 1)], 4: [("OT", 1)], 12: [("PV", 2)], 14: [("OT", 2)]}
        front_ = {1: [("MS", 1)], 2: [("RR", 1)], 3: [("GG", 1)], 4: [("DD", 0), ("CS", 1)], 6: [("HL", 1)]}
        maxima = [("M", 0, q, k) for q in range(2) for k in range(FILLS)]
        for k in range(2 * FILLS):
            b(("S", 1, k // FILLS, k % FILLS))
            for s in front_.get(k, []):
                f(s)
            for s in behind.get(k, []):
                b(s)
            if k >= 7:
                f(maxima.pop(0))
                if not (k - 7) % 3:
                    f(maxima.pop(0))
        f(("DM", 1)), f(("ST", 0, 0)), b(("PV", 3)), f(maxima.pop(0)), f(("V",)), b(("OT", 3)), f(("DD", 1))
        for s in maxima:
            f(s)
        b(("AT",)), f(("ST", 0, 1)), f(("DN",)), b(("OP",)), f(("Y",))
        return seq

    with ExitStack() as ctx:
        def sb(name, shape, dt=F32):
            return ctx.enter_context(nc.sbuf_tensor(name, shape, dt))

        def ps(name, shape):
            return ctx.enter_context(nc.psum_tensor(name, shape, F32))

        def sem(name):
            return ctx.enter_context(nc.semaphore(name))

        ps_s = ps("ps_s", [P, 2, 512])
        ps_m = ps("ps_m", [P, 2, 512])
        ps_o = ps("ps_o", [P, 512])
        ps_t = ps("ps_t", [P, 512])
        ps_w = ps("ps_w", [P, 2, 512])

        KH, Q, KL = range(3)
        stacks = sb("stacks", [P, U, HU, 3, S], F16)
        probs = sb("probs", [P, 2, QH * TRI])
        part_hi = sb("part_hi", [P, NF, 2, S], F16)
        part_lo = sb("part_lo", [P, NF, 2, S], F16)
        feat_t = sb("feat_t", [P, U, 2, S])
        feat_w = sb("feat_w", [P, 2, S])
        feat_a = sb("feat_a", [P, U, 2, S])
        feat_s = sb("feat_s", [P, U, 2, S])
        feat_c = sb("feat_c", [P, U, 2, S])
        x_in = sb("x_in", [P, NT, D])
        xn = sb("xn", [P, NT, D])
        x_hi = sb("x_hi", [P, C, S], F16)
        x_lo = sb("x_lo", [P, C, S], F16)
        v_sb = sb("v_sb", [P, NT, H, HD + 1])
        attn = sb("attn", [P, NT, D])
        y_sb = sb("y_sb", [P, NT, D])
        h_hi = sb("h_hi", [P, NH, S], F16)
        h_lo = sb("h_lo", [P, NH, S], F16)
        o_sb = xn[:].rearrange("p a b -> p (a b)")[:, 0:S]
        w_qkv = sb("w_qkv", [P, 5, 2, C, D], F16)
        w_o = sb("w_o", [P, 2, C, D], F16)
        w_gu = sb("w_gu", [P, 2, 2, C, HID], F16)
        w_d = sb("w_d", [P, 2, NH, D], F16)
        ident = sb("ident", [P, P])
        big_ident = sb("big_ident", [P, P], F16)
        mask_t = sb("mask_t", [P, P], F16)
        mask_m = sb("mask_m", [P, P], F16)
        same_head = sb("same_head", [P, P])
        lam = sb("lam", [P, U])
        stats = sb("stats", [P, NT, 6])
        mean_var = sb("mean_var", [P, NT, 2])
        rstd = sb("rstd", [P, NT])
        newton = sb("newton", [P, NT])
        neg_max = sb("neg_max", [P, 2, NT, QH])
        shift = sb("shift", [QH, 2, S], F16)
        recip = sb("recip", [P, NT, QH])
        ao_hi = feat_w[:].rearrange("p a b -> p (a b)").bitcast(F16)[:, 0:C * S].rearrange("p (c s) -> p c s", c=C)
        ao_lo = feat_w[:].rearrange("p a b -> p (a b)").bitcast(F16)[:, C * S:2 * C * S].rearrange("p (c s) -> p c s", c=C)

        loaded, consts, cleared, converted = sem("loaded"), sem("consts"), sem("cleared"), sem("converted")
        turned, split_done, lam_done = sem("turned"), sem("split_done"), sem("lam_done")

        per = {}

        def step_sem(name, n):
            s = sem(name)
            per[id(s)] = n
            return s

        x_loaded = step_sem("x_loaded", 16)
        ln_stats, ln_aggr, ln_root, ln_newton, ln_done = (step_sem(n, k) for n, k in (
            ("ln_stats", NT), ("ln_aggr", NT), ("ln_root", 2), ("ln_newton", 3), ("ln_done", NT)))
        ln_newton_end = step_sem("ln_newton_end", 1)
        xt_ready, xhi_ready, xlo_ready = (step_sem(n, 1) for n in ("xt_ready", "xhi_ready", "xlo_ready"))
        abs_ready, e_ready, l_ready, a_ready, sq_ready = (step_sem(n, 2) for n in (
            "abs_ready", "e_ready", "l_ready", "a_ready", "sq_ready"))
        qk_ready, t_ready, pp_ready, th_ready = (step_sem(n, 4) for n in ("qk_ready", "t_ready", "pp_ready", "th_ready"))
        ms_ready, msln_ready, r_ready = (step_sem(n, 2) for n in ("ms_ready", "msln_ready", "r_ready"))
        g_ready = step_sem("g_ready", 4)
        abst_ready, cos_ready, sin_ready = (step_sem(n, 2) for n in (
            "abst_ready", "cos_ready", "sin_ready"))
        cs_ready, hi_ready, lo_ready = (step_sem(n, k) for n, k in (("cs_ready", 4), ("hi_ready", 2 * NF), ("lo_ready", 2 * NF)))
        NDMA = NF * 2
        stacked, doubled = step_sem("stacked", 16 * NDMA * U), step_sem("doubled", 16 * 2 * U)
        max_filled = [step_sem(f"max_filled{j}", 2 * FILLS) for j in range(U)]
        max_read = [step_sem(f"max_read{j}", 2 * FILLS) for j in range(U)]
        turned_max = [step_sem(f"turned_max{j}", 2) for j in range(U)]
        shift_ready = [step_sem(f"shift_ready{j}", 2) for j in range(U)]
        shift_stored = [[step_sem(f"shift_stored{j}{q}", 16) for q in range(2)] for j in range(U)]
        v_ready, v_stored = step_sem("v_ready", 1), step_sem("v_stored", 1)
        gate_ready, up_ready, silu_ready, h_ready, hhi_ready, hlo_ready = (step_sem(n, NH) for n in (
            "gate_ready", "up_ready", "silu_ready", "h_ready", "hhi_ready", "hlo_ready"))
        down_ready, y_ready = step_sem("down_ready", 1), step_sem("y_ready", 1)
        s_filled, exp_done = step_sem("s_filled", 4 * FILLS), step_sem("exp_done", 4 * FILLS)
        pv_done, o_copied, o_turned, o_recip, o_normed = (step_sem(n, 4) for n in (
            "pv_done", "o_copied", "o_turned", "o_recip", "o_normed"))
        at_ready, aohi_ready, aolo_ready, op_ready, res_ready = (step_sem(n, 1) for n in (
            "at_ready", "aohi_ready", "aolo_ready", "op_ready", "res_ready"))
        stored = step_sem("stored", 16)
        gate = sem("gate")

        def now(s, i, c):
            return i * per[id(s)] + c

        def past(s, i, c):
            return i * per[id(s)] + (c - per[id(s)])

        def w_released(user, z):
            n = user[1] if len(user) > 1 else 0
            return {"T": (xlo_ready, 1), "QK": (t_ready, 2 * n + z + 1), "PP": (th_ready, 2 * n + z + 1), "MS": (msln_ready, n + 1),
                    "FG": ((silu_ready, h_ready)[z], n + 1), "V": (v_stored, 1), "AT": (aolo_ready, 1), "OP": (res_ready, 1)}[user[0]]

        def swapped(v):
            return bass.AP(v.tensor, v.offset + S, [v.ap[0], [-S, 2], [1, S]])

        block = ctx.enter_context(nc.Block())

        def steps_of(eng, emit):
            emit(0, schedule(True, False), first=True)
            with eng.Fori(1, B) as i:
                emit(i, schedule(True, True))
            emit(B, schedule(False, True))

        raw_w = probs[:, 0, :]
        raw = [raw_w[:, n * C * D:(n + 1) * C * D].rearrange("p (c d) -> p c d", c=C) for n in range(6)]
        off = 6 * C * D
        flat = probs[:].rearrange("p a b -> p (a b)")
        raw_g = [flat[:, off + n * NH * D:off + (n + 1) * NH * D] for n in range(2)]
        raw_d = flat[:, off + 2 * NH * D:off + 3 * NH * D]

        @block.sync
        def _(sp):
            for n, w in enumerate((wq, wk, wqp, wkp, wv, wo)):
                sp.dma_start(raw[n], w.rearrange("(c p) d -> p c d", p=P)).then_inc(loaded, 16)
            for n, w in enumerate((w_gate, w_up)):
                sp.dma_start(raw_g[n].bitcast(I32).rearrange("p (n d) -> p n d", n=NH),
                             w.rearrange("(n p) d -> p n d", p=P)).then_inc(loaded, 16)
            sp.dma_start(raw_d.bitcast(I32).rearrange("p (c n) -> p c n", c=C),
                         w_down.rearrange("(c p) n -> p c n", p=P)).then_inc(loaded, 16)
            for j in range(U):
                src = bass.AP(lam_raw.tensor, j * HU, [[0, HD], [1, HU], [1, 1]])
                sp.dma_start(lam[:, j:j + 1], src).then_inc(loaded, 16)

            def emit(i, steps, first=False):
                front = ("LN",) in steps
                back = ("AT",) in steps

                for s in steps:
                    if s[0] == "LN":
                        if not first:
                            sp.wait_ge(y_ready, past(y_ready, i, 1))
                            sp.sem_inc(gate, 1)
                        sp.dma_start(x_in[:], x[i].rearrange("(t p) d -> p t d", p=P)).then_inc(x_loaded, 16)
                    elif s[0] == "DM":
                        j = s[1]
                        sp.wait_ge(hi_ready, now(hi_ready, i, NF * (j + 1)))
                        sp.sem_inc(gate, 1)
                        sp.wait_ge(lo_ready, now(lo_ready, i, NF * (j + 1)))
                        sp.sem_inc(gate, 1)
                        if back:
                            sp.wait_ge(s_filled, now(s_filled, i, 2 * FILLS * (j + 1)))
                            sp.sem_inc(gate, 1)
                        for m in range(NF):
                            r = HD * m
                            sp.dma_start(stacks[r:r + HD, j, :, KH:Q + 1, :].rearrange("p h a t -> p h (a t)"),
                                         part_hi[:, m].rearrange("p a t -> p (a t)")).then_inc(stacked, 16)
                            sp.dma_start(stacks[R + r:R + r + HD, j, :, Q:KL + 1, :].rearrange("p h a t -> p h (a t)"),
                                         part_lo[:, m].rearrange("p a t -> p (a t)")).then_inc(stacked, 16)
                    elif s[0] == "DD":
                        j = s[1]
                        sp.wait_ge(stacked, now(stacked, i, 16 * NDMA * (j + 1)))
                        sp.sem_inc(gate, 1)
                        sp.dma_start(stacks[R:2 * R, j, :, KH, :], stacks[0:R, j, :, KH, :]).then_inc(doubled, 16)
                        sp.dma_start(stacks[0:R, j, :, KL, :], stacks[R:2 * R, j, :, KL, :]).then_inc(doubled, 16)
                    elif s[0] == "ST":
                        _, j, q = s
                        sp.wait_ge(shift_ready[j], now(shift_ready[j], i, q + 1))
                        sp.sem_inc(gate, 1)
                        sp.dma_start(stacks[2 * R:2 * R + 1, j, QH * q:QH * q + QH, Q, :],
                                     shift[:, q, :]).then_inc(shift_stored[j][q], 16)
                    elif s[0] == "OP":
                        sp.wait_ge(res_ready, now(res_ready, i, 1))
                        sp.sem_inc(gate, 1)
                        sp.dma_start(out[i - 1].rearrange("(t p) d -> p t d", p=P), attn[:]).then_inc(stored, 16)

            steps_of(sp, emit)
            sp.wait_ge(stored, 16 * (B + 1))

        @block.gpsimd
        def _(pool):
            pool.memset(ident[:], 0.0).then_inc(consts, 1)
            pool.memset(big_ident[:], 0.0).then_inc(consts, 1)
            pool.memset(mask_t[:], 0.0).then_inc(consts, 1)
            pool.memset(mask_m[:], 0.0).then_inc(consts, 1)
            pool.memset(same_head[:], 0.0).then_inc(consts, 1)
            pool.memset(v_sb[:], 1.0).then_inc(consts, 1)
            pool.wait_ge(consts, 6)
            pool.affine_select(out=ident[:], in_=ident[:], compare_op=ALU.not_equal, fill=1.0, base=0,
                               pattern=[[-1, P]], channel_multiplier=1).then_inc(consts, 1)
            pool.affine_select(out=big_ident[:], in_=big_ident[:], compare_op=ALU.not_equal, fill=BIG, base=0,
                               pattern=[[-1, P]], channel_multiplier=1).then_inc(consts, 1)
            pool.affine_select(out=mask_t[:], in_=mask_t[:], compare_op=ALU.is_ge, fill=-BIG, base=0,
                               pattern=[[1, P]], channel_multiplier=-1).then_inc(consts, 1)
            pool.affine_select(out=mask_m[:], in_=mask_m[:], compare_op=ALU.is_ge, fill=-BIG, base=0,
                               pattern=[[-1, P]], channel_multiplier=1).then_inc(consts, 1)
            for e in range(-(HD - 1), HD):
                pool.affine_select(out=same_head[:], in_=same_head[:], compare_op=ALU.not_equal, fill=1.0, base=-HU * e,
                                   pattern=[[-1, P]], channel_multiplier=1).then_inc(consts, 1)
                pool.wait_ge(consts, 11 + e + HD - 1)
            for s, k in ((s_filled, 1), (exp_done, 1), (pv_done, 1), (o_copied, 1), (o_turned, 1), (o_recip, 1),
                         (o_normed, 1), (at_ready, 1), (aohi_ready, 1), (aolo_ready, 1), (op_ready, 1),
                         (res_ready, 1), (stored, 1), (max_filled[1], 1), (max_read[1], 1), (turned_max[1], 1),
                         (shift_ready[1], 1), (shift_stored[1][0], 1), (shift_stored[1][1], 1)):
                pool.sem_inc(s, per[id(s)])

            def emit(i, steps, first=False):
                for s in steps:
                    if s[0] == "HL":
                        j = s[1]
                        if j:
                            pool.wait_ge(stacked, now(stacked, i, 16 * NDMA))
                            pool.sem_inc(gate, 1)
                        elif not first:
                            pool.wait_ge(stacked, past(stacked, i, 32 * NDMA))
                            pool.sem_inc(gate, 1)
                        pool.wait_ge(t_ready, now(t_ready, i, 2 * j + 2))
                        pool.sem_inc(gate, 1)
                        for m, src in enumerate((feat_t, feat_c, feat_s)):
                            if m:
                                pool.wait_ge(cs_ready, now(cs_ready, i, 2 * j + m))
                                pool.sem_inc(gate, 1)
                            pool.tensor_scalar(swapped(part_hi[:, m]), src[:, j], 1.0, 0.0, ALU.mult, ALU.add).then_inc(hi_ready, 1)

            steps_of(pool, emit)

        @block.scalar
        def _(act):
            act.preload_act_table_set(TRIG_SET)
            act.wait_ge(loaded, 16 * 11)
            act.activation(lam[:], lam[:], ACT.Tanh).then_inc(lam_done, 1)
            act.preload_act_table_set(EXP_SET)

            def emit(i, steps, first=False):
                for s in steps:
                    k = s[0]
                    if k == "LN":
                        act.wait_ge(ln_aggr, now(ln_aggr, i, NT))
                        act.activation(rstd[:], mean_var[:, :, 1], ACT.Ln, bias=NORM_EPS).then_inc(ln_root, 1)
                        act.wait_ge(ln_root, now(ln_root, i, 1))
                        act.activation(rstd[:], rstd[:], ACT.Exp, scale=-0.5).then_inc(ln_root, 1)
                    elif k == "T":
                        act.wait_ge(xt_ready, now(xt_ready, i, 1))
                        act.activation(x_hi[:], ps_w[:], ACT.Copy).then_inc(xhi_ready, 1)
                    elif k == "QK":
                        j = s[1]
                        if not first:
                            act.wait_ge(lo_ready, past(lo_ready, i, NF * j + 1))
                        for z in range(2):
                            act.wait_ge(qk_ready, now(qk_ready, i, 2 * j + z + 1))
                            act.activation(feat_t[:, j, z], ps_w[:, z], ACT.Copy, scale=1.0 / W_SCALE).then_inc(t_ready, 1)
                    elif k == "EL":
                        j = s[1]
                        act.wait_ge(abs_ready, now(abs_ready, i, j + 1))
                        act.activation(feat_w[:], feat_w[:], ACT.Exp, scale=-1.0).then_inc(e_ready, 1)
                        act.wait_ge(e_ready, now(e_ready, i, j + 1))
                        act.activation(feat_w[:], feat_w[:], ACT.Ln, bias=1.0).then_inc(l_ready, 1)
                    elif k == "SQ":
                        j = s[1]
                        act.wait_ge(a_ready, now(a_ready, i, j + 1))
                        act.activation(feat_w[:], feat_a[:, j], ACT.Square).then_inc(sq_ready, 1)
                    elif k == "RR":
                        j = s[1]
                        act.wait_ge(ms_ready, now(ms_ready, i, j + 1))
                        act.activation(feat_w[:], ps_w[:], ACT.Ln, scale=1.0 / HD, bias=AMP_EPS).then_inc(msln_ready, 1)
                        act.wait_ge(msln_ready, now(msln_ready, i, j + 1))
                        act.activation(feat_w[:], feat_w[:], ACT.Exp, scale=-0.5).then_inc(r_ready, 1)
                    elif k == "TRIG":
                        act.preload_act_table_set(TRIG_SET)
                    elif k == "EXPS":
                        act.preload_act_table_set(EXP_SET)
                    elif k == "PP":
                        j = s[1]
                        if not first:
                            act.wait_ge(lo_ready, past(lo_ready, i, NF * (j + 1)))
                        for z in range(2):
                            act.wait_ge(pp_ready, now(pp_ready, i, 2 * j + z + 1))
                            act.activation(feat_s[:, j, z], ps_w[:, z], ACT.Tanh, scale=1.0 / W_SCALE).then_inc(th_ready, 1)
                    elif k == "SC":
                        j = s[1]
                        act.wait_ge(abst_ready, now(abst_ready, i, j + 1))
                        act.activation(feat_c[:, j], feat_c[:, j], ACT.Sin, scale=-pi, bias=pi / 2).then_inc(cos_ready, 1)
                        act.activation(feat_s[:, j], feat_s[:, j], ACT.Sin, scale=pi).then_inc(sin_ready, 1)
                    elif k == "FG":
                        n = s[1]
                        act.wait_ge(gate_ready, now(gate_ready, i, n + 1))
                        if n >= 2:
                            act.wait_ge(hlo_ready, now(hlo_ready, i, n - 1))
                        elif not first:
                            act.wait_ge(op_ready, past(op_ready, i, 1))
                        act.activation(feat_w[:, n % 2], ps_w[:, 0], ACT.Silu, scale=DEQ).then_inc(silu_ready, 1)
                    elif k == "S":
                        _, w, q, f = s
                        n = (2 * w + q) * FILLS + f
                        act.wait_ge(s_filled, now(s_filled, i, n + 1))
                        if f == 0:
                            act.wait_ge(pv_done, now(pv_done, i, 2 * w + q - 1))
                        c0 = (f // 5) * 2 * TRI + P_PLACE[f % 5]
                        act.activation(probs[:, q, c0:c0 + 512], ps_s[:, f % 2], ACT.Exp, scale=SCORE).then_inc(exp_done, 1)
                    elif k == "OT":
                        q = s[1]
                        act.wait_ge(pv_done, now(pv_done, i, q + 1))
                        act.wait_ge(o_turned, now(o_turned, i, q))
                        act.activation(o_sb, ps_o[:], ACT.Copy).then_inc(o_copied, 1)
                    elif k == "AT":
                        act.wait_ge(at_ready, now(at_ready, i, 1))
                        if ("GG", 1) in steps:
                            act.wait_ge(g_ready, now(g_ready, i, 4))
                        else:
                            act.wait_ge(op_ready, past(op_ready, i, 1))
                        act.activation(ao_hi, ps_w[:], ACT.Copy).then_inc(aohi_ready, 1)

            steps_of(act, emit)

        @block.vector
        def _(dve):
            dve.wait_ge(loaded, 16 * 11)
            dve.memset(ps_o[:], 0.0).then_inc(cleared, 1)
            dve.memset(stacks[2 * R:2 * R + 1, :, :, KH, :], SHIFT).then_inc(cleared, 1)
            done = 0

            def two(hi, lo, src, scale=1.0):
                nonlocal done
                dve.tensor_scalar(hi, src, scale, None, ALU.mult).then_inc(split_done, 1)
                dve.wait_ge(split_done, done + 1)
                dve.scalar_tensor_tensor(lo, src, scale, hi, ALU.mult, ALU.subtract).then_inc(split_done, 1)
                done += 2

            for n in range(4):
                for c in range(C):
                    for j in range(U):
                        cols = slice(j * P, (j + 1) * P)
                        view = raw[n][:, c, cols].rearrange("p (h d) -> p d h", d=HD)
                        hi, lo = (w_qkv[:, n, z, c, cols].rearrange("p (d h) -> p d h", h=HU) for z in range(2))
                        two(hi, lo, view, W_SCALE)
            two(w_qkv[:, 4, 0], w_qkv[:, 4, 1], raw[4], W_SCALE)
            two(w_o[:, 0], w_o[:, 1], raw[5], W_SCALE)
            for w in (*raw_g, raw_d):
                dve.tensor_copy(w, w.bitcast(I32)).then_inc(converted, 1)
            for g in range(2):
                for c in range(C):
                    for half in range(2):
                        k = (g * C + c) * 2 + half
                        dve.wait_ge(turned, k + 1)
                        cols = slice(half * 384, half * 384 + 384)
                        two(w_gu[:, g, 0, c, cols], w_gu[:, g, 1, c, cols], ps_w[:, half, 0:384])
            for n in range(NH):
                dve.wait_ge(turned, 8 + n + 1)
                two(w_d[:, 0, n], w_d[:, 1, n], ps_w[:, n % 2, 0:D])
            dve.wait_ge(lam_done, 1)
            dve.tensor_scalar(lam[:], lam[:], 0.5, None, ALU.mult).then_inc(lam_done, 1)

            def emit(i, steps, first=False):
                for s in steps:
                    k = s[0]
                    if k == "LN":
                        dve.wait_ge(x_loaded, now(x_loaded, i, 16))
                        for t in range(NT):
                            dve.bn_stats(stats[:, t], x_in[:, t]).then_inc(ln_stats, 1)
                        for t in range(NT):
                            dve.wait_ge(ln_stats, now(ln_stats, i, t + 1))
                            dve.sem_inc(gate, 1)
                            dve.bn_aggr(mean_var[:, t], stats[:, t]).then_inc(ln_aggr, 1)
                        dve.wait_ge(ln_root, now(ln_root, i, 2))
                        dve.tensor_tensor(newton[:], rstd[:], rstd[:], ALU.mult).then_inc(ln_newton, 1)
                        dve.wait_ge(ln_aggr, now(ln_aggr, i, NT))
                        dve.wait_ge(ln_newton, now(ln_newton, i, 1))
                        dve.scalar_tensor_tensor(newton[:], mean_var[:, :, 1], NORM_EPS, newton[:], ALU.add, ALU.mult).then_inc(ln_newton, 1)
                        dve.wait_ge(ln_newton, now(ln_newton, i, 2))
                        dve.tensor_scalar(newton[:], newton[:], -0.5, 1.5, ALU.mult, ALU.add).then_inc(ln_newton, 1)
                        dve.wait_ge(ln_newton, now(ln_newton, i, 3))
                        dve.tensor_tensor(rstd[:], rstd[:], newton[:], ALU.mult).then_inc(ln_newton_end, 1)
                        dve.wait_ge(ln_newton_end, now(ln_newton_end, i, 1))
                        if not first:
                            dve.wait_ge(xt_ready, past(xt_ready, i, 1))
                            dve.wait_ge(o_turned, past(o_turned, i, 4))
                        for t in range(NT):
                            dve.tensor_scalar(xn[:, t], x_in[:, t], mean_var[:, t, 0:1], rstd[:, t:t + 1],
                                              ALU.subtract, ALU.mult).then_inc(ln_done, 1)
                    elif k == "T":
                        dve.wait_ge(xhi_ready, now(xhi_ready, i, 1))
                        dve.tensor_tensor(x_lo[:], ps_w[:], x_hi[:], ALU.subtract).then_inc(xlo_ready, 1)
                    elif k == "AB":
                        j = s[1]
                        dve.wait_ge(t_ready, now(t_ready, i, 2 * j + 2))
                        if j:
                            dve.wait_ge(g_ready, now(g_ready, i, 2))
                        else:
                            dve.wait_ge(hlo_ready, now(hlo_ready, i, NH))
                        dve.tensor_scalar(feat_w[:].bitcast(I32), feat_t[:, j].bitcast(I32), ABS_BITS, None, ALU.bitwise_and).then_inc(abs_ready, 1)
                    elif k == "AA":
                        j = s[1]
                        dve.wait_ge(l_ready, now(l_ready, i, j + 1))
                        if not first:
                            dve.wait_ge(cs_ready, past(cs_ready, i, 2 * j + 2))
                        dve.scalar_tensor_tensor(feat_a[:, j], feat_t[:, j], 0.0, feat_w[:], ALU.max, ALU.add).then_inc(a_ready, 1)
                    elif k == "GG":
                        j = s[1]
                        dve.wait_ge(r_ready, now(r_ready, i, j + 1))
                        dve.wait_ge(sq_ready, now(sq_ready, i, j + 1))
                        dve.tensor_tensor(feat_a[:, j, 0], feat_a[:, j, 0], feat_w[:, 0], ALU.mult).then_inc(g_ready, 1)
                        dve.scalar_tensor_tensor(feat_a[:, j, 1], feat_a[:, j, 1], lam[:, j:j + 1], feat_w[:, 1],
                                                 ALU.mult, ALU.mult).then_inc(g_ready, 1)
                    elif k == "PP":
                        j = s[1]
                        dve.wait_ge(th_ready, now(th_ready, i, 2 * j + 2))
                        if not first:
                            dve.wait_ge(lo_ready, past(lo_ready, i, NF * j + 2))
                        dve.tensor_scalar(feat_c[:, j].bitcast(I32), feat_s[:, j].bitcast(I32), ABS_BITS, None, ALU.bitwise_and).then_inc(abst_ready, 1)
                    elif k == "CS":
                        j = s[1]
                        dve.wait_ge(g_ready, now(g_ready, i, 2 * j + 2))
                        dve.wait_ge(cos_ready, now(cos_ready, i, j + 1))
                        dve.tensor_tensor(feat_c[:, j], feat_c[:, j], feat_a[:, j], ALU.mult).then_inc(cs_ready, 1)
                        dve.wait_ge(sin_ready, now(sin_ready, i, j + 1))
                        dve.tensor_tensor(feat_s[:, j], feat_s[:, j], feat_a[:, j], ALU.mult).then_inc(cs_ready, 1)
                    elif k == "HL":
                        j = s[1]
                        for m, src in enumerate((feat_t, feat_c, feat_s)):
                            dve.wait_ge(hi_ready, now(hi_ready, i, NF * j + m + 1))
                            if m:
                                dve.wait_ge(cs_ready, now(cs_ready, i, 2 * j + m))
                            dve.tensor_tensor(part_lo[:, m], src[:, j], swapped(part_hi[:, m]), ALU.subtract).then_inc(lo_ready, 1)
                    elif k == "M":
                        _, j, q, f = s
                        n = q * FILLS + f
                        dve.wait_ge(max_filled[j], now(max_filled[j], i, n + 1))
                        if f == 0:
                            if j == 0:
                                dve.wait_ge(turned_max[1], now(turned_max[1], i, q + 1))
                            else:
                                if not first:
                                    dve.wait_ge(turned_max[0], past(turned_max[0], i, q + 1))
                        pair = 2 * (f // 5)
                        fill = M_FILL[f % 5]
                        if f % 5 == 4:
                            dve.tensor_reduce(neg_max[:, q, 1, pair:pair + 2], ps_m[:, f % 2].rearrange("p (h c) -> p h c", h=2),
                                              AX_X, ALU.max, negate=True).then_inc(max_read[j], 1)
                        else:
                            for z, (h2, qt, col, width) in enumerate(fill):
                                ins = dve.tensor_reduce(neg_max[:, q, qt, pair + h2:pair + h2 + 1], ps_m[:, f % 2, col:col + width],
                                                        AX_X, ALU.max, negate=True)
                                if z == len(fill) - 1:
                                    ins.then_inc(max_read[j], 1)
                    elif k == "ST":
                        _, j, q = s
                        dve.wait_ge(turned_max[j], now(turned_max[j], i, q + 1))
                        if j == 0:
                            dve.wait_ge(shift_stored[1][q], now(shift_stored[1][q], i, 16))
                        else:
                            if not first:
                                dve.wait_ge(shift_stored[0][q], past(shift_stored[0][q], i, 16))
                        dve.tensor_scalar(shift[:, q], ps_t[0:QH, :], 1.0 / SHIFT, None, ALU.mult).then_inc(shift_ready[j], 1)
                    elif k == "OT":
                        q = s[1]
                        dve.wait_ge(o_turned, now(o_turned, i, q + 1))
                        dve.wait_ge(o_normed, now(o_normed, i, q))
                        v = ps_t[:].rearrange("p (t c e) -> p t c e", t=NT, c=QH)
                        dve.reciprocal(recip[:], v[:, :, :, HD]).then_inc(o_recip, 1)
                        dve.wait_ge(o_recip, now(o_recip, i, q + 1))
                        if q == 0:
                            if not first:
                                dve.wait_ge(stored, past(stored, i, 16))
                        o = attn[:, :, QH * HD * q:QH * HD * (q + 1)].rearrange("p t (c d) -> p t c d", c=QH)
                        r = recip[:].unsqueeze(3).to_broadcast([P, NT, QH, HD])
                        dve.tensor_tensor(o, v[:, :, :, 0:HD], r, ALU.mult).then_inc(o_normed, 1)
                    elif k == "AT":
                        dve.wait_ge(aohi_ready, now(aohi_ready, i, 1))
                        dve.tensor_tensor(ao_lo, ps_w[:], ao_hi, ALU.subtract).then_inc(aolo_ready, 1)
                    elif k == "OP":
                        dve.wait_ge(op_ready, now(op_ready, i, 1))
                        if not first:
                            dve.wait_ge(y_ready, past(y_ready, i, 1))
                        dve.scalar_tensor_tensor(attn[:], ps_w[:].rearrange("p a (b d) -> p (a b) d", d=D), 1.0 / W_SCALE, y_sb[:],
                                                 ALU.mult, ALU.add).then_inc(res_ready, 1)
                    elif k == "V":
                        dve.wait_ge(v_ready, now(v_ready, i, 1))
                        dve.wait_ge(pv_done, now(pv_done, i, 4))
                        dve.tensor_scalar(v_sb[:, :, :, 0:HD], ps_w[:].rearrange("p a (b h d) -> p (a b) h d", b=2, d=HD),
                                          1.0 / W_SCALE, None, ALU.mult).then_inc(v_stored, 1)
                    elif k == "FG":
                        n = s[1]
                        dve.wait_ge(silu_ready, now(silu_ready, i, n + 1))
                        dve.wait_ge(up_ready, now(up_ready, i, n + 1))
                        dve.scalar_tensor_tensor(feat_w[:, n % 2], ps_w[:, 1], DEQ / H_SCALE, feat_w[:, n % 2], ALU.mult, ALU.mult).then_inc(h_ready, 1)
                        dve.wait_ge(h_ready, now(h_ready, i, n + 1))
                        if n == 0:
                            if not first:
                                dve.wait_ge(down_ready, past(down_ready, i, 1))
                        dve.tensor_copy(h_hi[:, n], feat_w[:, n % 2]).then_inc(hhi_ready, 1)
                        dve.wait_ge(hhi_ready, now(hhi_ready, i, n + 1))
                        dve.tensor_tensor(h_lo[:, n], feat_w[:, n % 2], h_hi[:, n], ALU.subtract).then_inc(hlo_ready, 1)
                    elif k == "Y":
                        dve.wait_ge(down_ready, now(down_ready, i, 1))
                        dve.wait_ge(res_ready, now(res_ready, i, 1))
                        dve.scalar_tensor_tensor(y_sb[:], ps_m[:].rearrange("p a (b d) -> p (a b) d", d=D), DEQ * H_SCALE, x_in[:],
                                                 ALU.mult, ALU.add).then_inc(y_ready, 1)

            steps_of(dve, emit)

        @block.tensor
        def _(pe):
            pe.wait_ge(consts, 6 + 4 + 2 * HD - 1)
            pe.wait_ge(cleared, 2)
            k = 0
            for g in range(2):
                pe.wait_ge(converted, g + 1)
                for c in range(C):
                    for half in range(2):
                        if k >= 2:
                            pe.wait_ge(split_done, 2 * (4 * C * U + 2) + 2 * (k - 1))
                        for n in range(3):
                            m = half * 3 + n
                            ins = pe.transpose(ps_w[:, half, n * P:(n + 1) * P], raw_g[g][:, m * D + c * P:m * D + c * P + P], ident[:])
                        ins.then_inc(turned, 1)
                        k += 1
            pe.wait_ge(converted, 3)
            for n in range(NH):
                pe.wait_ge(split_done, 2 * (4 * C * U + 2) + 2 * (k - 1))
                for c in range(C):
                    ins = pe.transpose(ps_w[:, n % 2, c * P:(c + 1) * P], raw_d[:, c * HID + n * P:c * HID + n * P + P], ident[:])
                ins.then_inc(turned, 1)
                k += 1
            pe.wait_ge(split_done, 2 * (4 * C * U + 2) + 2 * k)

            HI, LO = 0, 1
            PRODUCTS = ((HI, HI), (LO, HI), (HI, LO))
            xp, hp, aop = (x_hi, x_lo), (h_hi, h_lo), (ao_hi, ao_lo)

            def emit(i, steps, first=False):
                back = ("AT",) in steps
                users = [s for s in steps if s[0] in ("T", "QK", "PP", "MS", "FG", "V", "AT", "OP")]

                def take_w(s, *banks):
                    at = users.index(s)
                    if at:
                        for r, c in dict(w_released(users[at - 1], z) for z in banks).items():
                            pe.wait_ge(r, now(r, i, c))
                    elif not first:
                        pe.wait_ge(res_ready, past(res_ready, i, 1))
                        pe.wait_ge(v_stored, past(v_stored, i, 1))

                def project(n, j, qk):
                    k = 0
                    for c in range(C):
                        for wx, xx in PRODUCTS:
                            ins = pe.matmul(ps_w[:, qk], w_qkv[:, n, wx, c, j * P:(j + 1) * P], xp[xx][:, c],
                                            start=(k == 0), stop=(k == 3 * C - 1))
                            k += 1
                    return ins

                def tokens_major(out, left, right, chunks):
                    for t in range(NT):
                        k = 0
                        for c in range(chunks):
                            for lx, rx in PRODUCTS:
                                ins = pe.matmul(out[:, t // 2, (t % 2) * D:(t % 2 + 1) * D], left[lx][:, c, t * P:(t + 1) * P],
                                                right(rx, c), start=(k == 0), stop=(k == 3 * chunks - 1))
                                k += 1
                    return ins

                for s in steps:
                    k = s[0]
                    if k in ("T", "MS", "V", "AT", "OP"):
                        take_w(s, 0, 1)
                    if k == "T":
                        pe.wait_ge(ln_done, now(ln_done, i, NT))
                        for c in range(C):
                            for t in range(NT):
                                ins = pe.transpose(ps_w[:, c, t * P:(t + 1) * P], xn[:, t, c * P:(c + 1) * P], ident[:])
                        ins.then_inc(xt_ready, 1)
                    elif k == "QK":
                        j = s[1]
                        pe.wait_ge(xlo_ready, now(xlo_ready, i, 1))
                        for z in range(2):
                            take_w(s, z)
                            project(z, j, z).then_inc(qk_ready, 1)
                    elif k == "PP":
                        j = s[1]
                        for z in range(2):
                            take_w(s, z)
                            project(2 + z, j, z).then_inc(pp_ready, 1)
                    elif k == "MS":
                        j = s[1]
                        pe.wait_ge(sq_ready, now(sq_ready, i, j + 1))
                        for z in range(2):
                            ins = pe.matmul(ps_w[:, z], same_head[:], feat_w[:, z], start=True, stop=True)
                        ins.then_inc(ms_ready, 1)
                    elif k == "V":
                        tokens_major(ps_w, xp, lambda r, c: w_qkv[:, 4, r, c], C).then_inc(v_ready, 1)
                    elif k == "FG":
                        n = s[1]
                        for g in range(2):
                            take_w(s, g)
                            k2 = 0
                            for c in range(C):
                                for wx, xx in PRODUCTS:
                                    ins = pe.matmul(ps_w[:, g], w_gu[:, g, wx, c, n * P:(n + 1) * P], xp[xx][:, c],
                                                    start=(k2 == 0), stop=(k2 == 3 * C - 1))
                                    k2 += 1
                            ins.then_inc((gate_ready, up_ready)[g], 1)
                    elif k == "DN":
                        pe.wait_ge(hlo_ready, now(hlo_ready, i, NH))
                        pe.wait_ge(max_read[0], now(max_read[0], i, 2 * FILLS))
                        tokens_major(ps_m, hp, lambda r, c: w_d[:, r, c], NH).then_inc(down_ready, 1)
                    elif k == "AT":
                        pe.wait_ge(o_normed, now(o_normed, i, 4))
                        for c in range(C):
                            for t in range(NT):
                                ins = pe.transpose(ps_w[:, c, t * P:(t + 1) * P], attn[:, t, c * P:(c + 1) * P], ident[:])
                        ins.then_inc(at_ready, 1)
                    elif k == "OP":
                        pe.wait_ge(aolo_ready, now(aolo_ready, i, 1))
                        tokens_major(ps_w, aop, lambda r, c: w_o[:, r, c], C).then_inc(op_ready, 1)
                    elif k == "M":
                        _, j, q, f = s
                        n = q * FILLS + f
                        if f == 0:
                            if j == 0:
                                pe.wait_ge(doubled, now(doubled, i, 32))
                            else:
                                pe.wait_ge(doubled, past(doubled, i, 64))
                        if n >= 2:
                            pe.wait_ge(max_read[j], now(max_read[j], i, n - 1))
                        elif j == 0:
                            pe.wait_ge(max_read[1], now(max_read[1], i, 2 * FILLS - 1 + n))
                        else:
                            pe.wait_ge(max_read[0], past(max_read[0], i, 2 * FILLS - 1 + n))
                            pe.wait_ge(y_ready, past(y_ready, i, 1))
                        for h2, qt, col, width in M_FILL[f % 5]:
                            head = QH * q + 2 * (f // 5) + h2
                            o = ps_m[:, f % 2, col:col + width]
                            pe.matmul(o, stacks[0:2 * R, j, head, Q, qt * P:(qt + 1) * P], stacks[0:2 * R, j, head, KH, 0:width],
                                      start=True, stop=False)
                            ins = pe.matmul(ps_m[:, f % 2, col + width - P:col + width], big_ident[:], mask_m[:], start=False, stop=True)
                        ins.then_inc(max_filled[j], 1)
                    elif k == "ST":
                        _, j, q = s
                        pe.wait_ge(max_read[j], now(max_read[j], i, FILLS * (q + 1)))
                        take_t(i, s, steps, first)
                        for t in range(NT):
                            ins = pe.transpose(ps_t[0:QH, t * P:(t + 1) * P], neg_max[:, q, t], ident[:])
                        ins.then_inc(turned_max[j], 1)
                    elif k == "S":
                        _, w, q, f = s
                        n = (2 * w + q) * FILLS + f
                        if f == 0:
                            if w == 0:
                                if not first:
                                    pe.wait_ge(shift_stored[0][q], past(shift_stored[0][q], i, 16))
                            else:
                                pe.wait_ge(shift_stored[1][q], now(shift_stored[1][q], i, 16))
                        if n >= 2:
                            pe.wait_ge(exp_done, now(exp_done, i, n - 1))
                        else:
                            if not first:
                                pe.wait_ge(exp_done, past(exp_done, i, 4 * FILLS - 1 + n))
                        for h2, kt, col, width in S_FILL[f % 5]:
                            head = QH * q + 2 * (f // 5) + h2
                            o = ps_s[:, f % 2, col:col + width]
                            keys, queries = slice(kt * P, (kt + 1) * P), slice(kt * P, S)
                            pe.matmul(o, stacks[0:2 * R + 1, w, head, KH, keys], stacks[0:2 * R + 1, w, head, Q, queries], start=True, stop=False)
                            pe.matmul(o, stacks[0:2 * R, w, head, KL, keys], stacks[0:2 * R, w, head, Q, queries], start=False, stop=False)
                            ins = pe.matmul(ps_s[:, f % 2, col:col + P], big_ident[:], mask_t[:], start=False, stop=True)
                        ins.then_inc(s_filled, 1)
                    elif k == "PV":
                        qd = s[1]
                        pe.wait_ge(exp_done, now(exp_done, i, FILLS * (qd + 1)))
                        pe.wait_ge(o_copied, now(o_copied, i, qd))
                        if qd == 0:
                            if not first:
                                pe.wait_ge(v_stored, past(v_stored, i, 1))
                        for kt in range(NT):
                            for c in range(QH):
                                c0 = p_columns(c, kt)
                                ins = pe.matmul(ps_o[32 * c:32 * c + HD + 1, kt * P:S], v_sb[:, kt, QH * qd + c, :],
                                                probs[:, qd % 2, c0:c0 + S - kt * P], start=(kt == 0), stop=(kt == NT - 1))
                        ins.then_inc(pv_done, 1)
                    elif k == "OT":
                        q = s[1]
                        pe.wait_ge(o_copied, now(o_copied, i, q + 1))
                        take_t(i, s, steps, first)
                        for t in range(NT):
                            ins = pe.transpose(ps_t[:, t * P:(t + 1) * P], o_sb[:, t * P:(t + 1) * P], ident[:])
                        ins.then_inc(o_turned, 1)

            def take_t(i, s, steps, first):
                users = [u for u in steps if u[0] in ("ST", "OT")]
                at = users.index(s)
                if at:
                    u = users[at - 1]
                    if u[0] == "ST":
                        pe.wait_ge(shift_ready[u[1]], now(shift_ready[u[1]], i, u[2] + 1))
                    else:
                        pe.wait_ge(o_normed, now(o_normed, i, u[1] + 1))
                else:
                    if not first:
                        pe.wait_ge(shift_ready[0], past(shift_ready[0], i, 2))
                    if not first:
                        pe.wait_ge(o_normed, past(o_normed, i, 4))

            steps_of(pe, emit)


_INS = ['L0_attn_x', 'L0_attn_Wq', 'L0_attn_Wk', 'L0_attn_Wv', 'L0_attn_Wo', 'L0_attn_Wqp', 'L0_attn_Wkp',
        'L0_attn_lambda_raw', 'L0_ffn_w_gate', 'L0_ffn_w_up', 'L0_ffn_w_down']


def kernel(**inputs):
    import numpy as _np
    import concourse.bacc as _bacc
    from concourse import mybir as _mybir
    from concourse.bass_utils import run_bass_kernel_spmd as _run

    nc = _bacc.Bacc("TRN2", target_bir_lowering=False, num_devices=1)
    arrays, args = {}, []
    for name in _INS:
        a = _np.ascontiguousarray(inputs[name])
        arrays[f"in_{name}"] = a
        args.append(nc.dram_tensor(f"in_{name}", a.shape, _mybir.dt.from_np(a.dtype), kind="ExternalInput").ap())
    shape = inputs['L0_attn_x'].shape
    out = nc.dram_tensor("out_0", shape, _mybir.dt.float32, kind="ExternalOutput").ap()
    phase_attention_and_ffn(nc, *args, out)
    r = _run(nc, [arrays], core_ids=[0])
    return r.results[0]["out_0"]
```

```python
from contextlib import ExitStack
from math import pi

import concourse.bass as bass
from concourse import mybir

F32 = mybir.dt.float32
F16 = mybir.dt.float16
I32 = mybir.dt.int32
ALU = mybir.AluOpType
ACT = mybir.ActivationFunctionType
AX_X = mybir.AxisListType.X

P = 128
BIG = 60000.0
W_SCALE = 16.0
SHIFT = 16.0
ABS_BITS = 0x7FFFFFFF
H_SCALE = 16.0
EXP_SET = "natural_log_exp_and_others"
TRIG_SET = "silu_and_others"


def phase_attention_and_ffn(nc, x, wq, wk, wv, wo, wqp, wkp, lam_raw, w_gate, w_up, w_down, out):
    B, S, D = x.shape
    HID = w_gate.shape[0]
    H = lam_raw.shape[0]
    HD = D // H
    NT = S // P
    C = D // P
    NH = HID // P
    U = 2
    HU = H // U
    QH = 4
    NF = 3
    R = NF * HD
    TRI = P * NT * (NT + 1) // 2
    FILLS = 10
    NORM_EPS, AMP_EPS = 1e-5, 1e-6
    SCORE = float(HD) ** -0.5
    DEQ = 1.0 / 127.0

    S_FILL = [[(0, 0, 0, 512)], [(0, 1, 0, 384), (0, 3, 384, 128)],
              [(1, 0, 0, 512)], [(1, 1, 0, 384), (1, 3, 384, 128)],
              [(0, 2, 0, 256), (1, 2, 256, 256)]]
    M_FILL = [[(0, 3, 0, 512)], [(0, 2, 0, 384), (0, 0, 384, 128)],
              [(1, 3, 0, 512)], [(1, 2, 0, 384), (1, 0, 384, 128)],
              [(0, 1, 0, 256), (1, 1, 256, 256)]]
    P_PLACE = [0, 512, 1024, 1536, 2048]

    def p_columns(head, kt):
        pair, hp = head // 2, head % 2
        for f, fill in enumerate(S_FILL):
            for (h2, t2, col, _) in fill:
                if (h2, t2) == (hp, kt):
                    return pair * 2 * TRI + P_PLACE[f] + col

    FIRST = """
        LR LS LX W:0 W:1 W:2 T QK:0 AB:0 CV WT:0 EL:0 AA:0 SQ:0 QK:1 WT:1 W:3 WT:2 MS:0 WT:3 RR:0 HL:0.0 DM:0.0 GG:0
        AB:1 WT:4 EL:1 W:4 WT:5 WT:6 AA:1 SQ:1 WT:7 W:5 MS:1 WT:8 RR:1 TRIG WT:9 GG:1 PP:0 SC:0.1 CS:0.1 PP:1 SC:0.2
        HL:0.1 DM:0.1 FG:0 CS:0.2 HL:0.2 DM:0.2 FG:1 DD:0 HH:0 SC:1.1 HH:1 FG:2 HH:2 SC:1.2 CS:1.1 FG:3 CS:1.2
        HL:1.0 DM:1.0 HH:3 FG:4 HH:4 FG:5 V M:0.0.0 M:0.0.1 M:0.0.2 M:0.0.3 M:0.0.4 M:0.0.5 M:0.0.6 HH:5 EXPS
        M:0.0.7 WT:10 M:0.0.8 WT:11 M:0.0.9 NS:0.0 WT:12 WT:13 LW:0 HL:1.1 M:0.1.0 DM:1.1 M:0.1.1 ST:0.0 LW:1 DN:0
        M:0.1.2 M:0.1.3 HL:1.2 DN:1 DM:1.2 M:0.1.4 M:0.1.5 M:0.1.6 DN:2 M:0.1.7 Y:0 LK DN:3 M:0.1.8 M:0.1.9 NS:0.1
        DD:1 Y:1 YM ST:0.1"""
    LOOP = """
        M:1.0.0 M:1.0.1 S:0.0.0 S:0.0.1 S:0.0.2 S:0.0.3 LR LS M:1.0.2 M:1.0.3 S:0.0.4 M:1.0.4 S:0.0.5 M:1.0.5
        S:0.0.6 LX M:1.0.6 S:0.0.7 M:1.0.7 S:0.0.8 S:0.0.9 M:1.0.8 M:1.0.9 NS:1.0 T OC:0 PV:0 TRIG ST:1.0 QK:0 QK:1
        PP:0 PP:1 SC:0.1 SC:0.2 FG:0 FG:1 OT:0 SC:1.1 HH:0 HH:1 FG:2 SC:1.2 HH:2 FG:3 FG:4 HH:3 HH:4 FG:5 HH:5 EXPS
        S:0.1.0 M:1.1.0 M:1.1.1 S:0.1.1 S:0.1.2 EL:0 AB:0 M:1.1.2 S:0.1.3 M:1.1.3 M:1.1.4 S:0.1.4 AA:0 SQ:0 S:0.1.5
        M:1.1.5 S:0.1.6 M:1.1.6 MS:0 M:1.1.7 S:0.1.7 S:0.1.8 M:1.1.8 M:1.1.9 NS:1.1 RR:0 GG:0 S:0.1.9 AB:1 CS:0.1
        CS:0.2 S:1.0.0 EL:1 DN:0 S:1.0.1 SQ:1 DN:1 DN:2 HL:0.0 DM:0.0 AA:1 HL:0.1 DM:0.1 S:1.0.2 HL:0.2 DM:0.2 DN:3
        ST:1.1 S:1.0.3 OC:1 PV:1 S:1.0.4 Y:0 S:1.0.5 Y:1 S:1.0.6 S:1.0.7 S:1.0.8 S:1.0.9 MS:1 OT:1 GG:1 RR:1 CS:1.1
        S:1.1.0 DD:0 CS:1.2 HL:1.0 HL:1.1 HL:1.2 S:1.1.1 OC:2 PV:2 S:1.1.2 AT:0 S:1.1.3 S:1.1.4 M:0.0.0 M:0.0.1
        S:1.1.5 M:0.0.2 M:0.0.3 OT:2 M:0.0.4 S:1.1.6 M:0.0.5 M:0.0.6 S:1.1.7 S:1.1.8 M:0.0.7 M:0.0.8 S:1.1.9 M:0.0.9
        NS:0.0 M:0.1.0 M:0.1.1 ST:0.0 PV:3 OC:3 DM:1.0 DM:1.1 DM:1.2 M:0.1.2 M:0.1.3 V OT:3 M:0.1.4 DD:1 M:0.1.5 YM
        AT:1 M:0.1.6 M:0.1.7 M:0.1.8 M:0.1.9 NS:0.1 OP ST:0.1"""
    LAST = """
        M:1.0.0 M:1.0.1 S:0.0.0 S:0.0.1 S:0.0.2 S:0.0.3 M:1.0.2 M:1.0.3 S:0.0.4 M:1.0.4 S:0.0.5 S:0.0.6 M:1.0.5
        M:1.0.6 S:0.0.7 S:0.0.8 M:1.0.7 S:0.0.9 M:1.0.8 M:1.0.9 NS:1.0 PV:0 OC:0 ST:1.0 OT:0 S:0.1.0 M:1.1.0 M:1.1.1
        S:0.1.1 M:1.1.2 S:0.1.2 M:1.1.3 S:0.1.3 S:0.1.4 M:1.1.4 M:1.1.5 S:0.1.5 S:0.1.6 M:1.1.6 S:0.1.7 M:1.1.7
        S:0.1.8 M:1.1.8 S:0.1.9 S:1.0.0 M:1.1.9 NS:1.1 S:1.0.1 S:1.0.2 ST:1.1 S:1.0.3 OC:1 PV:1 S:1.0.4 S:1.0.5
        S:1.0.6 S:1.0.7 OT:1 S:1.0.8 S:1.0.9 S:1.1.0 S:1.1.1 S:1.1.2 OC:2 PV:2 S:1.1.3 S:1.1.4 S:1.1.5 S:1.1.6 OT:2
        S:1.1.7 S:1.1.8 S:1.1.9 PV:3 OC:3 OT:3 AT:0 AT:1 OP"""

    def pieces(order):
        return [(kind, *(int(n) for n in numbers.split(".") if n))
                for kind, _, numbers in (token.partition(":") for token in order.split())]

    with ExitStack() as ctx:
        def sb(name, shape, dt=F32):
            return ctx.enter_context(nc.sbuf_tensor(name, shape, dt))

        def ps(name, shape):
            return ctx.enter_context(nc.psum_tensor(name, shape, F32))

        def sem(name):
            return ctx.enter_context(nc.semaphore(name))

        ps_s = ps("ps_s", [P, 2, 512])
        ps_m = ps("ps_m", [P, 2, 512])
        ps_o = ps("ps_o", [P, 512])
        ps_t = ps("ps_t", [P, 512])
        ps_w = ps("ps_w", [P, 2, 512])

        KH, Q, KL = range(3)
        stacks = sb("stacks", [P, U, HU, 3, S], F16)
        probs = sb("probs", [P, 2, QH * TRI])
        part_hi = sb("part_hi", [P, NF, 2, S], F16)
        part_lo = sb("part_lo", [P, NF, 2, S], F16)
        feat_t = sb("feat_t", [P, U, 2, S])
        feat_w = sb("feat_w", [P, 2, S])
        feat_a = sb("feat_a", [P, 2, S])
        feat_s = sb("feat_s", [P, U, 2, S])
        feat_c = sb("feat_c", [P, U, 2, S])
        x_in = sb("x_in", [P, NT, D])
        xn = sb("xn", [P, NT, D])
        x_hi = sb("x_hi", [P, C, S], F16)
        x_lo = sb("x_lo", [P, C, S], F16)
        v_sb = sb("v_sb", [P, NT, H, HD + 1])
        attn = sb("attn", [P, NT, D])
        y_sb = sb("y_sb", [P, NT, D])
        h_hi = sb("h_hi", [P, NH, S], F16)
        h_lo = sb("h_lo", [P, NH, S], F16)
        o_sb = sb("o_sb", [P, S])
        w_qkv = sb("w_qkv", [P, 5, 2, C, D], F16)
        w_o = sb("w_o", [P, 2, C, D], F16)
        w_gu = sb("w_gu", [P, 2, 2, C, HID], F16)
        w_d = sb("w_d", [P, 2, NH, D], F16)
        ident = sb("ident", [P, P])
        big_ident = sb("big_ident", [P, P], F16)
        mask_t = sb("mask_t", [P, P], F16)
        mask_m = sb("mask_m", [P, P], F16)
        same_head = sb("same_head", [P, P])
        lam = sb("lam", [P, U])
        stats = sb("stats", [P, NT, 6])
        mean_var = sb("mean_var", [P, NT, 2])
        rstd = sb("rstd", [P, NT])
        newton = sb("newton", [P, NT])
        neg_max = sb("neg_max", [P, 2, NT, QH])
        neg_shift = sb("neg_shift", [P, 2, NT, QH], F16)
        shift = sb("shift", [QH, 2, S], F16)
        low = sb("low", [P, 2 * C + NH + 1])
        low_seen = sb("low_seen", [1, 1], I32)
        recip = sb("recip", [P, NT, QH])
        ao_hi = feat_w[:].rearrange("p a b -> p (a b)").bitcast(F16)[:, 0:C * S].rearrange("p (c s) -> p c s", c=C)
        ao_lo = feat_w[:].rearrange("p a b -> p (a b)").bitcast(F16)[:, C * S:2 * C * S].rearrange("p (c s) -> p c s", c=C)

        w_loaded = [sem(f"w_loaded{n}") for n in range(6)]
        ffn_loaded = [sem(f"ffn_loaded{n}") for n in range(3)]
        converted = [sem(f"converted{n}") for n in range(3)]
        x0_loaded = sem("x0_loaded")
        lam_loaded, lam_done, ident_ready, masks_ready = sem("lam_loaded"), sem("lam_done"), sem("ident_ready"), sem("masks_ready")
        ones_ready, cleared, same_ready = sem("ones_ready"), sem("cleared"), sem("same_ready")
        whi_ready, wlo_ready = sem("whi_ready"), sem("wlo_ready")
        turned, fhi_ready, flo_ready = sem("turned"), sem("fhi_ready"), sem("flo_ready")

        per = {}

        def step_sem(name, n):
            s = sem(name)
            per[id(s)] = n
            return s

        x_loaded, residual_loaded, y_moved = (step_sem(n, 16) for n in ("x_loaded", "residual_loaded", "y_moved"))
        ln_stats, ln_aggr, ln_root, ln_newton, ln_done = (step_sem(n, k) for n, k in (
            ("ln_stats", NT), ("ln_aggr", NT), ("ln_root", 2), ("ln_newton", 3), ("ln_done", NT)))
        ln_newton_end = step_sem("ln_newton_end", 1)
        xt_ready, xhi_ready, xlo_ready = (step_sem(n, 1) for n in ("xt_ready", "xhi_ready", "xlo_ready"))
        abs_ready, e_ready, l_ready, a_ready, sq_ready = (step_sem(n, 2) for n in (
            "abs_ready", "e_ready", "l_ready", "a_ready", "sq_ready"))
        qk_ready, t_ready, pp_ready, th_ready = (step_sem(n, 4) for n in ("qk_ready", "t_ready", "pp_ready", "th_ready"))
        ms_ready, msln_ready, r_ready = (step_sem(n, 2) for n in ("ms_ready", "msln_ready", "r_ready"))
        g_ready = step_sem("g_ready", 4)
        abst_ready, cos_ready, sin_ready = (step_sem(n, 2) for n in (
            "abst_ready", "cos_ready", "sin_ready"))
        cs_ready, hi_ready, lo_ready = (step_sem(n, k) for n, k in (("cs_ready", 4), ("hi_ready", 2 * NF), ("lo_ready", 2 * NF)))
        NDMA = NF * 2
        stacked, doubled = step_sem("stacked", 16 * NDMA * U), step_sem("doubled", 16 * 2 * U)
        max_filled = [step_sem(f"max_filled{j}", 2 * FILLS) for j in range(U)]
        max_read = [step_sem(f"max_read{j}", 2 * FILLS) for j in range(U)]
        neg_ready = [step_sem(f"neg_ready{j}", 2) for j in range(U)]
        turned_max = [step_sem(f"turned_max{j}", 2) for j in range(U)]
        shift_ready = [step_sem(f"shift_ready{j}", 2) for j in range(U)]
        shift_stored = [[step_sem(f"shift_stored{j}{q}", 16) for q in range(2)] for j in range(U)]
        v_ready, v_stored = step_sem("v_ready", 1), step_sem("v_stored", 1)
        gate_ready, up_ready, silu_ready, h_ready, hhi_ready, hlo_ready = (step_sem(n, NH) for n in (
            "gate_ready", "up_ready", "silu_ready", "h_ready", "hhi_ready", "hlo_ready"))
        down_ready, y_ready = step_sem("down_ready", NT), step_sem("y_ready", 2)
        s_filled, exp_done = step_sem("s_filled", 4 * FILLS), step_sem("exp_done", 4 * FILLS)
        pv_done, o_copied, o_turned, o_recip, o_normed = (step_sem(n, 4) for n in (
            "pv_done", "o_copied", "o_turned", "o_recip", "o_normed"))
        at_ready, aohi_ready, aolo_ready = (step_sem(n, C) for n in ("at_ready", "aohi_ready", "aolo_ready"))
        op_ready, res_ready = (step_sem(n, 1) for n in ("op_ready", "res_ready"))
        stored = step_sem("stored", 16)
        low_summed, low_turned, low_known = sem("low_summed"), sem("low_turned"), sem("low_known")
        gate = sem("gate")

        def now(s, i, c):
            return i * per[id(s)] + c

        def past(s, i, c):
            return i * per[id(s)] + (c - per[id(s)])

        def w_released(user, z):
            n = user[1] if len(user) > 1 else 0
            return {"T": (xlo_ready, 1), "QK": (t_ready, 2 * n + z + 1), "PP": (th_ready, 2 * n + z + 1), "MS": (msln_ready, n + 1),
                    "FG": ((silu_ready, h_ready)[z], n + 1), "V": (v_stored, 1), "AT": (aolo_ready, n + 1), "OP": (res_ready, 1),
                    "DN": (y_ready, z + 1)}[user[0]]

        def hidden(n):
            return (ps_w, ps_s)[n % 2]

        def w_banks(user):
            return {"AT": user[1:], "DN": (user[-1] // 2,)}.get(user[0], (0, 1)) if len(user) > 1 else (0, 1)

        def amplitudes(j, first):
            return attn[:].rearrange("p t d -> p (t d)").rearrange("p (a s) -> p a s", a=2) if first and j else feat_a[:]

        def weight_parts(n):
            if n == 4:
                return [(w_qkv[:, 4, 0], w_qkv[:, 4, 1], raw[4])]
            if n == 5:
                return [(w_o[:, 0], w_o[:, 1], raw[5])]
            return [(*(w_qkv[:, n, z, c, j * P:(j + 1) * P].rearrange("p (d h) -> p d h", h=HU) for z in range(2)),
                     raw[n][:, c, j * P:(j + 1) * P].rearrange("p (h d) -> p d h", d=HD)) for c in range(C) for j in range(U)]

        def turned_parts(k):
            if k < 4 * C:
                half, g, c = k // (2 * C), k // C % 2, k % C
                n0 = half * NH // 2
                cols = slice(n0 * P, n0 * P + HID // 2)
                return w_gu[:, g, 0, c, cols], w_gu[:, g, 1, c, cols], [raw_g[g][:, (n0 + n) * D + c * P:(n0 + n) * D + c * P + P] for n in range(NH // 2)]
            n = k - 4 * C
            return w_d[:, 0, n], w_d[:, 1, n], [raw_d[:, c * HID + n * P:c * HID + n * P + P] for c in range(C)]

        def swapped(v):
            return bass.AP(v.tensor, v.offset + S, [v.ap[0], [-S, 2], [1, S]])

        block = ctx.enter_context(nc.Block())

        def steps_of(eng, emit):
            emit(0, pieces(FIRST), first=True)
            with eng.Fori(1, B) as i:
                emit(i, pieces(LOOP))
            emit(B, pieces(LAST))

        raw_w = probs[:, 0, :]
        raw = [raw_w[:, n * C * D:(n + 1) * C * D].rearrange("p (c d) -> p c d", c=C) for n in range(6)]
        off = 6 * C * D
        flat = probs[:].rearrange("p a b -> p (a b)")
        raw_g = [flat[:, off + n * NH * D:off + (n + 1) * NH * D] for n in range(2)]
        raw_d = flat[:, off + 2 * NH * D:off + 3 * NH * D]

        @block.sync
        def _(sp):
            sp.dma_start(xn[:], x[0].rearrange("(t p) d -> p t d", p=P)).then_inc(x0_loaded, 16)
            for n, w in enumerate((wq, wk, wqp, wkp, wv, wo)):
                sp.dma_start(raw[n], w.rearrange("(c p) d -> p c d", p=P)).then_inc(w_loaded[n], 16)

            def emit(i, steps, first=False):
                back = ("OP",) in steps

                for s in steps:
                    if s[0] == "LS":
                        if not first:
                            sp.wait_ge(y_moved, past(y_moved, i, 16))
                            sp.sem_inc(gate, 1)
                        sp.dma_start(x_in[:], x[i].rearrange("(t p) d -> p t d", p=P)).then_inc(residual_loaded, 16)
                    elif s[0] == "DM":
                        _, j, m = s
                        sp.wait_ge(hi_ready, now(hi_ready, i, NF * j + m + 1))
                        sp.sem_inc(gate, 1)
                        sp.wait_ge(lo_ready, now(lo_ready, i, NF * j + m + 1))
                        sp.sem_inc(gate, 1)
                        if m == 0 and back:
                            sp.wait_ge(s_filled, now(s_filled, i, 2 * FILLS * (j + 1)))
                            sp.sem_inc(gate, 1)
                        r = HD * m
                        sp.dma_start(stacks[r:r + HD, j, :, KH:Q + 1, :].rearrange("p h a t -> p h (a t)"),
                                     part_hi[:, m].rearrange("p a t -> p (a t)")).then_inc(stacked, 16)
                        sp.dma_start(stacks[R + r:R + r + HD, j, :, Q:KL + 1, :].rearrange("p h a t -> p h (a t)"),
                                     part_lo[:, m].rearrange("p a t -> p (a t)")).then_inc(stacked, 16)
                    elif s[0] == "DD":
                        j = s[1]
                        sp.wait_ge(stacked, now(stacked, i, 16 * NDMA * (j + 1)))
                        sp.sem_inc(gate, 1)
                        sp.dma_start(stacks[R:2 * R, j, :, KH, :], stacks[0:R, j, :, KH, :]).then_inc(doubled, 16)
                        sp.dma_start(stacks[0:R, j, :, KL, :], stacks[R:2 * R, j, :, KL, :]).then_inc(doubled, 16)
                    elif s[0] == "ST":
                        _, j, q = s
                        sp.wait_ge(shift_ready[j], now(shift_ready[j], i, q + 1))
                        sp.sem_inc(gate, 1)
                        sp.dma_start(stacks[2 * R:2 * R + 1, j, QH * q:QH * q + QH, Q, :],
                                     shift[:, q, :]).then_inc(shift_stored[j][q], 16)
                    elif s[0] == "OP":
                        sp.wait_ge(res_ready, now(res_ready, i, 1))
                        sp.sem_inc(gate, 1)
                        sp.dma_start(out[i - 1].rearrange("(t p) d -> p t d", p=P), attn[:]).then_inc(stored, 16)
                    elif s[0] == "YM":
                        sp.wait_ge(y_ready, now(y_ready, i, 2))
                        sp.sem_inc(gate, 1)
                        sp.wait_ge(res_ready, now(res_ready, i, 1))
                        sp.sem_inc(gate, 1)
                        sp.dma_start(y_sb[:], x_in[:]).then_inc(y_moved, 16)

            steps_of(sp, emit)
            sp.wait_ge(stored, 16 * (B + 1))

        @block.gpsimd
        def _(pool):
            pool.memset(ident[:], 0.0).then_inc(ident_ready, 1)
            pool.wait_ge(ident_ready, 1)
            pool.affine_select(out=ident[:], in_=ident[:], compare_op=ALU.not_equal, fill=1.0, base=0,
                               pattern=[[-1, P]], channel_multiplier=1).then_inc(ident_ready, 1)
            pool.memset(big_ident[:], 0.0).then_inc(masks_ready, 1)
            pool.memset(mask_t[:], 0.0).then_inc(masks_ready, 1)
            pool.memset(mask_m[:], 0.0).then_inc(masks_ready, 1)
            pool.wait_ge(masks_ready, 3)
            pool.affine_select(out=big_ident[:], in_=big_ident[:], compare_op=ALU.not_equal, fill=BIG, base=0,
                               pattern=[[-1, P]], channel_multiplier=1).then_inc(masks_ready, 1)
            pool.affine_select(out=mask_t[:], in_=mask_t[:], compare_op=ALU.is_ge, fill=-BIG, base=0,
                               pattern=[[1, P]], channel_multiplier=-1).then_inc(masks_ready, 1)
            pool.affine_select(out=mask_m[:], in_=mask_m[:], compare_op=ALU.is_ge, fill=-BIG, base=0,
                               pattern=[[-1, P]], channel_multiplier=1).then_inc(masks_ready, 1)
            pool.memset(v_sb[:], 1.0).then_inc(ones_ready, 1)
            for s, k in ((s_filled, 1), (exp_done, 1), (pv_done, 1), (o_copied, 1), (o_turned, 1), (o_recip, 1),
                         (o_normed, 1), (at_ready, 1), (aohi_ready, 1), (aolo_ready, 1), (op_ready, 1),
                         (res_ready, 1), (stored, 1), (max_filled[1], 1), (max_read[1], 1), (turned_max[1], 1), (neg_ready[1], 1),
                         (shift_ready[1], 1), (shift_stored[1][0], 1), (shift_stored[1][1], 1)):
                pool.sem_inc(s, per[id(s)])

            def emit(i, steps, first=False):
                for s in steps:
                    if s[0] == "LS":
                        if not first:
                            pool.wait_ge(xt_ready, past(xt_ready, i, 1))
                            pool.sem_inc(gate, 1)
                            pool.dma_start(xn[:], x[i].rearrange("(t p) d -> p t d", p=P)).then_inc(x_loaded, 16)
                    elif s[0] == "CV":
                        for n, w in ((1, raw_g[1]), (2, raw_d)):
                            pool.wait_ge(ffn_loaded[n], 16)
                            pool.tensor_copy(w, w.bitcast(I32)).then_inc(converted[n], 1)
                        pool.wait_ge(converted[2], 1)
                        pool.memset(stacks[2 * R:2 * R + 1, :, :, KH, :], SHIFT).then_inc(cleared, 1)
                        pool.wait_ge(cleared, 2)
                    elif s[0] == "CS":
                        _, j, m = s
                        if j == 1 and m == 1:
                            pool.wait_ge(g_ready, now(g_ready, i, 4))
                            pool.wait_ge(cos_ready, now(cos_ready, i, 2))
                            pool.tensor_tensor(feat_c[:, 1], feat_c[:, 1], amplitudes(1, first), ALU.mult).then_inc(cs_ready, 1)
                        elif j == 1:
                            pool.wait_ge(sin_ready, now(sin_ready, i, 2))
                            pool.tensor_tensor(feat_s[:, 1], feat_s[:, 1], amplitudes(1, first), ALU.mult).then_inc(cs_ready, 1)
                    elif s[0] == "HL":
                        _, j, m = s
                        if m == 0:
                            if j:
                                pool.wait_ge(stacked, now(stacked, i, 16 * NDMA))
                                pool.sem_inc(gate, 1)
                            elif not first:
                                pool.wait_ge(stacked, past(stacked, i, 32 * NDMA))
                                pool.sem_inc(gate, 1)
                            pool.wait_ge(t_ready, now(t_ready, i, 2 * j + 2))
                            pool.sem_inc(gate, 1)
                        else:
                            pool.wait_ge(cs_ready, now(cs_ready, i, 2 * j + m))
                            pool.sem_inc(gate, 1)
                        src = (feat_t, feat_c, feat_s)[m]
                        pool.tensor_scalar(swapped(part_hi[:, m]), src[:, j], 1.0, 0.0, ALU.mult, ALU.add).then_inc(hi_ready, 1)
                        if j:
                            pool.wait_ge(hi_ready, now(hi_ready, i, NF * j + m + 1))
                            pool.tensor_tensor(part_lo[:, m], src[:, j], swapped(part_hi[:, m]), ALU.subtract).then_inc(lo_ready, 1)

            steps_of(pool, emit)

        @block.scalar
        def _(act):
            act.preload_act_table_set(TRIG_SET)
            for j in range(U):
                src = bass.AP(lam_raw.tensor, j * HU, [[0, HD], [1, HU], [1, 1]])
                act.dma_start(lam[:, j:j + 1], src).then_inc(lam_loaded, 16)
            for n, w in enumerate((w_gate, w_up)):
                act.dma_start(raw_g[n].bitcast(I32).rearrange("p (n d) -> p n d", n=NH),
                              w.rearrange("(n p) d -> p n d", p=P)).then_inc(ffn_loaded[n], 16)
            act.dma_start(raw_d.bitcast(I32).rearrange("p (c n) -> p c n", c=C),
                          w_down.rearrange("(c p) n -> p c n", p=P)).then_inc(ffn_loaded[2], 16)
            act.wait_ge(lam_loaded, 32)
            act.activation(lam[:], lam[:], ACT.Tanh).then_inc(lam_done, 1)
            act.preload_act_table_set(EXP_SET)

            def emit(i, steps, first=False):
                for s in steps:
                    k = s[0]
                    if k == "W":
                        act.wait_ge(w_loaded[s[1]], 16)
                        parts = weight_parts(s[1])
                        for hi, _, src in parts:
                            ins = act.activation(hi, src, ACT.Copy, scale=W_SCALE)
                        ins.then_inc(whi_ready, 1)
                    elif k == "WT":
                        act.wait_ge(turned, s[1] + 1)
                        hi, _, src = turned_parts(s[1])
                        act.activation(hi, ps_s[:, s[1] % 2, 0:P * len(src)], ACT.Copy).then_inc(fhi_ready, 1)
                    elif k == "LR":
                        act.wait_ge(ln_aggr, now(ln_aggr, i, NT))
                        act.activation(rstd[:], mean_var[:, :, 1], ACT.Ln, bias=NORM_EPS).then_inc(ln_root, 1)
                        act.wait_ge(ln_root, now(ln_root, i, 1))
                        act.activation(rstd[:], rstd[:], ACT.Exp, scale=-0.5).then_inc(ln_root, 1)
                    elif k == "T":
                        act.wait_ge(xt_ready, now(xt_ready, i, 1))
                        act.activation(x_hi[:], ps_w[:], ACT.Copy).then_inc(xhi_ready, 1)
                    elif k == "QK":
                        j = s[1]
                        if not first:
                            act.wait_ge(lo_ready, past(lo_ready, i, NF * j + 1))
                        for z in range(2):
                            act.wait_ge(qk_ready, now(qk_ready, i, 2 * j + z + 1))
                            act.activation(feat_t[:, j, z], ps_w[:, z], ACT.Copy, scale=1.0 / W_SCALE).then_inc(t_ready, 1)
                    elif k == "EL":
                        j = s[1]
                        act.wait_ge(abs_ready, now(abs_ready, i, j + 1))
                        act.activation(feat_w[:], feat_w[:], ACT.Exp, scale=-1.0).then_inc(e_ready, 1)
                        act.wait_ge(e_ready, now(e_ready, i, j + 1))
                        act.activation(feat_w[:], feat_w[:], ACT.Ln, bias=1.0).then_inc(l_ready, 1)
                    elif k == "SQ":
                        j = s[1]
                        act.wait_ge(a_ready, now(a_ready, i, j + 1))
                        act.activation(feat_w[:], amplitudes(j, first), ACT.Square).then_inc(sq_ready, 1)
                    elif k == "RR":
                        j = s[1]
                        act.wait_ge(ms_ready, now(ms_ready, i, j + 1))
                        act.activation(feat_w[:], ps_w[:], ACT.Ln, scale=1.0 / HD, bias=AMP_EPS).then_inc(msln_ready, 1)
                        act.wait_ge(msln_ready, now(msln_ready, i, j + 1))
                        act.activation(feat_w[:], feat_w[:], ACT.Exp, scale=-0.5).then_inc(r_ready, 1)
                    elif k == "TRIG":
                        act.preload_act_table_set(TRIG_SET)
                    elif k == "EXPS":
                        act.preload_act_table_set(EXP_SET)
                    elif k == "PP":
                        j = s[1]
                        if not first:
                            act.wait_ge(lo_ready, past(lo_ready, i, NF * (j + 1)))
                        for z in range(2):
                            act.wait_ge(pp_ready, now(pp_ready, i, 2 * j + z + 1))
                            act.activation(feat_s[:, j, z], ps_w[:, z], ACT.Tanh, scale=1.0 / W_SCALE).then_inc(th_ready, 1)
                    elif k == "SC":
                        _, j, m = s
                        act.wait_ge(abst_ready, now(abst_ready, i, j + 1))
                        if m == 1:
                            act.activation(feat_c[:, j], feat_c[:, j], ACT.Sin, scale=-pi, bias=pi / 2).then_inc(cos_ready, 1)
                        else:
                            act.activation(feat_s[:, j], feat_s[:, j], ACT.Sin, scale=pi).then_inc(sin_ready, 1)
                    elif k == "FG":
                        n = s[1]
                        act.wait_ge(gate_ready, now(gate_ready, i, n + 1))
                        if n >= 2:
                            act.wait_ge(hlo_ready, now(hlo_ready, i, n - 1))
                        elif not first:
                            act.wait_ge(op_ready, past(op_ready, i, 1))
                        else:
                            act.wait_ge(g_ready, now(g_ready, i, 4))
                        act.activation(feat_w[:, n % 2], hidden(n)[:, 0], ACT.Silu, scale=DEQ).then_inc(silu_ready, 1)
                    elif k == "HH":
                        n = s[1]
                        if n == 0:
                            if not first:
                                act.wait_ge(down_ready, past(down_ready, i, NT))
                        act.wait_ge(h_ready, now(h_ready, i, n + 1))
                        act.activation(h_hi[:, n], feat_w[:, n % 2], ACT.Copy).then_inc(hhi_ready, 1)
                    elif k == "S":
                        _, w, q, f = s
                        n = (2 * w + q) * FILLS + f
                        act.wait_ge(s_filled, now(s_filled, i, n + 1))
                        if f == 0:
                            act.wait_ge(pv_done, now(pv_done, i, 2 * w + q - 1))
                        c0 = (f // 5) * 2 * TRI + P_PLACE[f % 5]
                        act.activation(probs[:, q, c0:c0 + 512], ps_s[:, f % 2], ACT.Exp, scale=SCORE).then_inc(exp_done, 1)
                    elif k == "OC":
                        q = s[1]
                        act.wait_ge(pv_done, now(pv_done, i, q + 1))
                        act.wait_ge(o_turned, now(o_turned, i, q))
                        act.activation(o_sb[:], ps_o[:], ACT.Copy).then_inc(o_copied, 1)
                    elif k == "AT":
                        c = s[1]
                        act.wait_ge(at_ready, now(at_ready, i, c + 1))
                        if ("GG", 1) in steps:
                            act.wait_ge(g_ready, now(g_ready, i, 4))
                        else:
                            act.wait_ge(op_ready, past(op_ready, i, 1))
                        act.activation(ao_hi[:, c], ps_w[:, c], ACT.Copy).then_inc(aohi_ready, 1)

            steps_of(act, emit)

        @block.vector
        def _(dve):
            dve.memset(ps_o[:], 0.0).then_inc(cleared, 1)
            dve.wait_ge(ident_ready, 2)
            dve.tensor_reduce(low[:, 0:HU], ident[:].rearrange("p (d h) -> p h d", h=HU), AX_X, ALU.add).then_inc(same_ready, 1)
            dve.wait_ge(same_ready, 1)
            dve.tensor_copy(same_head[:].rearrange("p (d h) -> p d h", h=HU),
                            low[:, 0:HU].unsqueeze(1).to_broadcast([P, HD, HU])).then_inc(same_ready, 1)

            def emit(i, steps, first=False):
                for s in steps:
                    k = s[0]
                    if k == "W":
                        dve.wait_ge(whi_ready, s[1] + 1)
                        for hi, lo, src in weight_parts(s[1]):
                            ins = dve.scalar_tensor_tensor(lo, src, W_SCALE, hi, ALU.mult, ALU.subtract)
                        ins.then_inc(wlo_ready, 1)
                    elif k == "CV":
                        dve.wait_ge(ffn_loaded[0], 16)
                        dve.tensor_copy(raw_g[0], raw_g[0].bitcast(I32)).then_inc(converted[0], 1)
                        dve.wait_ge(lam_done, 1)
                        dve.tensor_scalar(lam[:], lam[:], 0.5, None, ALU.mult).then_inc(lam_done, 1)
                    elif k == "WT":
                        dve.wait_ge(fhi_ready, s[1] + 1)
                        hi, lo, src = turned_parts(s[1])
                        dve.tensor_tensor(lo, ps_s[:, s[1] % 2, 0:P * len(src)], hi, ALU.subtract).then_inc(flo_ready, 1)
                    elif k == "LS":
                        if first:
                            dve.wait_ge(x0_loaded, 16)
                        else:
                            dve.wait_ge(x_loaded, past(x_loaded, i, 16))
                        for t in range(NT):
                            dve.bn_stats(stats[:, t], xn[:, t]).then_inc(ln_stats, 1)
                        for t in range(NT):
                            dve.wait_ge(ln_stats, now(ln_stats, i, t + 1))
                            dve.sem_inc(gate, 1)
                            dve.bn_aggr(mean_var[:, t], stats[:, t]).then_inc(ln_aggr, 1)
                    elif k == "LX":
                        dve.wait_ge(ln_root, now(ln_root, i, 2))
                        dve.tensor_tensor(newton[:], rstd[:], rstd[:], ALU.mult).then_inc(ln_newton, 1)
                        dve.wait_ge(ln_aggr, now(ln_aggr, i, NT))
                        dve.wait_ge(ln_newton, now(ln_newton, i, 1))
                        dve.scalar_tensor_tensor(newton[:], mean_var[:, :, 1], NORM_EPS, newton[:], ALU.add, ALU.mult).then_inc(ln_newton, 1)
                        dve.wait_ge(ln_newton, now(ln_newton, i, 2))
                        dve.tensor_scalar(newton[:], newton[:], -0.5, 1.5, ALU.mult, ALU.add).then_inc(ln_newton, 1)
                        dve.wait_ge(ln_newton, now(ln_newton, i, 3))
                        dve.tensor_tensor(rstd[:], rstd[:], newton[:], ALU.mult).then_inc(ln_newton_end, 1)
                        dve.wait_ge(ln_newton_end, now(ln_newton_end, i, 1))
                        dve.wait_ge(ln_stats, now(ln_stats, i, NT))
                        for t in range(NT):
                            dve.tensor_scalar(xn[:, t], xn[:, t], mean_var[:, t, 0:1], rstd[:, t:t + 1],
                                              ALU.subtract, ALU.mult).then_inc(ln_done, 1)
                    elif k == "T":
                        dve.wait_ge(xhi_ready, now(xhi_ready, i, 1))
                        dve.tensor_tensor(x_lo[:], ps_w[:], x_hi[:], ALU.subtract).then_inc(xlo_ready, 1)
                    elif k == "AB":
                        j = s[1]
                        dve.wait_ge(t_ready, now(t_ready, i, 2 * j + 2))
                        if j:
                            dve.wait_ge(g_ready, now(g_ready, i, 2))
                        elif not first:
                            dve.wait_ge(hlo_ready, now(hlo_ready, i, NH))
                        dve.tensor_scalar(feat_w[:].bitcast(I32), feat_t[:, j].bitcast(I32), ABS_BITS, None, ALU.bitwise_and).then_inc(abs_ready, 1)
                    elif k == "AA":
                        j = s[1]
                        dve.wait_ge(l_ready, now(l_ready, i, j + 1))
                        if not first:
                            dve.wait_ge(cs_ready, now(cs_ready, i, 2) if j else past(cs_ready, i, 4))
                        dve.scalar_tensor_tensor(amplitudes(j, first), feat_t[:, j], 0.0, feat_w[:], ALU.max, ALU.add).then_inc(a_ready, 1)
                    elif k == "GG":
                        j = s[1]
                        dve.wait_ge(r_ready, now(r_ready, i, j + 1))
                        dve.wait_ge(sq_ready, now(sq_ready, i, j + 1))
                        if first:
                            dve.wait_ge(lam_done, 2)
                        amp = amplitudes(j, first)
                        dve.tensor_tensor(amp[:, 0], amp[:, 0], feat_w[:, 0], ALU.mult).then_inc(g_ready, 1)
                        dve.scalar_tensor_tensor(amp[:, 1], amp[:, 1], lam[:, j:j + 1], feat_w[:, 1],
                                                 ALU.mult, ALU.mult).then_inc(g_ready, 1)
                    elif k == "PP":
                        j = s[1]
                        dve.wait_ge(th_ready, now(th_ready, i, 2 * j + 2))
                        if not first:
                            dve.wait_ge(lo_ready, past(lo_ready, i, NF * j + 2))
                        dve.tensor_scalar(feat_c[:, j].bitcast(I32), feat_s[:, j].bitcast(I32), ABS_BITS, None, ALU.bitwise_and).then_inc(abst_ready, 1)
                    elif k == "CS":
                        _, j, m = s
                        if j == 0 and m == 1:
                            dve.wait_ge(g_ready, now(g_ready, i, 2))
                            dve.wait_ge(cos_ready, now(cos_ready, i, 1))
                            dve.tensor_tensor(feat_c[:, 0], feat_c[:, 0], amplitudes(0, first), ALU.mult).then_inc(cs_ready, 1)
                        elif j == 0:
                            dve.wait_ge(sin_ready, now(sin_ready, i, 1))
                            dve.tensor_tensor(feat_s[:, 0], feat_s[:, 0], amplitudes(0, first), ALU.mult).then_inc(cs_ready, 1)
                    elif k == "HL":
                        _, j, m = s
                        if j == 0:
                            dve.wait_ge(hi_ready, now(hi_ready, i, m + 1))
                            if m:
                                dve.wait_ge(cs_ready, now(cs_ready, i, m))
                            dve.tensor_tensor(part_lo[:, m], (feat_t, feat_c, feat_s)[m][:, 0], swapped(part_hi[:, m]),
                                              ALU.subtract).then_inc(lo_ready, 1)
                    elif k == "M":
                        _, j, q, f = s
                        n = q * FILLS + f
                        dve.wait_ge(max_filled[j], now(max_filled[j], i, n + 1))
                        if f == 0:
                            if j == 0:
                                dve.wait_ge(turned_max[1], now(turned_max[1], i, q + 1))
                            else:
                                if not first:
                                    dve.wait_ge(turned_max[0], past(turned_max[0], i, q + 1))
                        pair = 2 * (f // 5)
                        fill = M_FILL[f % 5]
                        if f % 5 == 4:
                            dve.tensor_reduce(neg_max[:, q, 1, pair:pair + 2], ps_m[:, f % 2].rearrange("p (h c) -> p h c", h=2),
                                              AX_X, ALU.max, negate=True).then_inc(max_read[j], 1)
                        else:
                            for z, (h2, qt, col, width) in enumerate(fill):
                                ins = dve.tensor_reduce(neg_max[:, q, qt, pair + h2:pair + h2 + 1], ps_m[:, f % 2, col:col + width],
                                                        AX_X, ALU.max, negate=True)
                                if z == len(fill) - 1:
                                    ins.then_inc(max_read[j], 1)
                    elif k == "NS":
                        _, j, q = s
                        dve.wait_ge(max_read[j], now(max_read[j], i, FILLS * (q + 1)))
                        dve.tensor_scalar(neg_shift[:, q], neg_max[:, q], 1.0 / SHIFT, None, ALU.mult).then_inc(neg_ready[j], 1)
                    elif k == "ST":
                        _, j, q = s
                        dve.wait_ge(turned_max[j], now(turned_max[j], i, q + 1))
                        if j == 0:
                            dve.wait_ge(shift_stored[1][q], now(shift_stored[1][q], i, 16))
                        else:
                            if not first:
                                dve.wait_ge(shift_stored[0][q], past(shift_stored[0][q], i, 16))
                        dve.tensor_scalar(shift[:, q], ps_t[0:QH, :], 1.0 / BIG, None, ALU.mult).then_inc(shift_ready[j], 1)
                    elif k == "OT":
                        q = s[1]
                        dve.wait_ge(o_turned, now(o_turned, i, q + 1))
                        dve.wait_ge(o_normed, now(o_normed, i, q))
                        v = ps_t[:].rearrange("p (t c e) -> p t c e", t=NT, c=QH)
                        dve.reciprocal(recip[:], v[:, :, :, HD]).then_inc(o_recip, 1)
                        dve.wait_ge(o_recip, now(o_recip, i, q + 1))
                        if q == 0:
                            if not first:
                                dve.wait_ge(stored, past(stored, i, 16))
                        o = attn[:, :, QH * HD * q:QH * HD * (q + 1)].rearrange("p t (c d) -> p t c d", c=QH)
                        r = recip[:].unsqueeze(3).to_broadcast([P, NT, QH, HD])
                        dve.tensor_tensor(o, v[:, :, :, 0:HD], r, ALU.mult).then_inc(o_normed, 1)
                    elif k == "AT":
                        c = s[1]
                        dve.wait_ge(aohi_ready, now(aohi_ready, i, c + 1))
                        dve.tensor_tensor(ao_lo[:, c], ps_w[:, c], ao_hi[:, c], ALU.subtract).then_inc(aolo_ready, 1)
                    elif k == "OP":
                        dve.wait_ge(op_ready, now(op_ready, i, 1))
                        if not first:
                            dve.wait_ge(y_moved, past(y_moved, i, 16))
                        dve.wait_ge(o_normed, now(o_normed, i, 4))
                        dve.scalar_tensor_tensor(attn[:], ps_w[:].rearrange("p a (b d) -> p (a b) d", d=D), 1.0 / W_SCALE, y_sb[:],
                                                 ALU.mult, ALU.add).then_inc(res_ready, 1)
                    elif k == "V":
                        dve.wait_ge(v_ready, now(v_ready, i, 1))
                        if first:
                            dve.wait_ge(ones_ready, 1)
                        dve.wait_ge(pv_done, now(pv_done, i, 4))
                        dve.tensor_scalar(v_sb[:, :, :, 0:HD], ps_w[:].rearrange("p a (b h d) -> p (a b) h d", b=2, d=HD),
                                          1.0 / W_SCALE, None, ALU.mult).then_inc(v_stored, 1)
                    elif k == "FG":
                        n = s[1]
                        dve.wait_ge(silu_ready, now(silu_ready, i, n + 1))
                        dve.wait_ge(up_ready, now(up_ready, i, n + 1))
                        dve.scalar_tensor_tensor(feat_w[:, n % 2], hidden(n)[:, 1], DEQ / H_SCALE, feat_w[:, n % 2], ALU.mult, ALU.mult).then_inc(h_ready, 1)
                    elif k == "HH":
                        n = s[1]
                        if n == 0:
                            if not first:
                                dve.wait_ge(down_ready, past(down_ready, i, NT))
                        dve.wait_ge(hhi_ready, now(hhi_ready, i, n + 1))
                        dve.tensor_tensor(h_lo[:, n], feat_w[:, n % 2], h_hi[:, n], ALU.subtract).then_inc(hlo_ready, 1)
                    elif k == "Y":
                        z = s[1]
                        dve.wait_ge(down_ready, now(down_ready, i, 2 * z + 2))
                        dve.wait_ge(residual_loaded, now(residual_loaded, i, 16))
                        half = x_in[:, 2 * z:2 * z + 2]
                        dve.scalar_tensor_tensor(half, ps_w[:, z].rearrange("p (b d) -> p b d", d=D), DEQ * H_SCALE, half,
                                                 ALU.mult, ALU.add).then_inc(y_ready, 1)

                    elif k == "LW":
                        last = 2 * C + NH
                        if s[1] == 0:
                            dve.wait_ge(flo_ready, 4 * C)
                            dve.tensor_reduce(low[:, 0:2 * C].rearrange("p (g c) -> p g c", g=2), w_gu[:, :, 1].bitcast(I32), AX_X, ALU.max,
                                              apply_absolute_value=True).then_inc(low_summed, 1)
                        else:
                            dve.wait_ge(flo_ready, 4 * C + NH)
                            dve.tensor_reduce(low[:, 2 * C:last], w_d[:, 1].bitcast(I32), AX_X, ALU.max,
                                              apply_absolute_value=True).then_inc(low_summed, 1)
                            dve.wait_ge(low_summed, 2)
                            dve.tensor_reduce(low[:, last:last + 1], low[:, 0:last], AX_X, ALU.max).then_inc(low_summed, 1)
                    elif k == "LK":
                        dve.wait_ge(low_turned, 1)
                        dve.tensor_reduce(low[0:1, 0:1], ps_t[0:1, 0:P], AX_X, ALU.max).then_inc(low_summed, 1)
                        dve.wait_ge(low_summed, 4)
                        dve.tensor_scalar(low_seen[:], low[0:1, 0:1], 1.0, None, ALU.min).then_inc(low_known, 1)

            steps_of(dve, emit)

        @block.tensor
        def _(pe):
            pe.wait_ge(ident_ready, 2)
            pe.wait_ge(cleared, 1)

            HI, LO = 0, 1
            PRODUCTS = ((HI, HI), (HI, LO), (LO, HI))
            xp, hp, aop = (x_hi, x_lo), (h_hi, h_lo), (ao_hi, ao_lo)

            def emit(i, steps, first=False, whole=True):
                ffn_products = PRODUCTS if whole else PRODUCTS[0:2]
                back = ("OP",) in steps
                users = [s for s in steps if s[0] in ("T", "QK", "PP", "MS", "V", "AT", "OP", "DN") or (s[0] == "FG" and s[1] % 2 == 0)]
                s_users = [s for s in steps if s[0] in ("S", "WT") or (s[0] == "FG" and s[1] % 2)]

                def take_w(s, *banks):
                    before = {z: [u for u in users[:users.index(s)] if z in w_banks(u)][-1:] for z in banks}
                    if before[banks[0]]:
                        for r, c in dict(w_released(before[z][0], z) for z in banks).items():
                            pe.wait_ge(r, now(r, i, c))
                    elif not first:
                        pe.wait_ge(res_ready, past(res_ready, i, 1))
                        pe.wait_ge(v_stored, past(v_stored, i, 1))

                def take_s(s, bank):
                    before = [u for u in s_users[:s_users.index(s)] if u[0] == "FG" or u[-1] % 2 == bank][-1:]
                    for u in before:
                        if u[0] == "S":
                            pe.wait_ge(exp_done, now(exp_done, i, (2 * u[1] + u[2]) * FILLS + u[3] + 1))
                        elif u[0] == "WT":
                            pe.wait_ge(flo_ready, u[1] + 1)
                        elif bank == 0:
                            pe.wait_ge(silu_ready, now(silu_ready, i, u[1] + 1))
                        else:
                            pe.wait_ge(h_ready, now(h_ready, i, u[1] + 1))
                    if not before and not first:
                        pe.wait_ge(exp_done, past(exp_done, i, 4 * FILLS - 1 + bank))

                def project(n, j, qk):
                    k = 0
                    for c in range(C):
                        for wx, xx in PRODUCTS:
                            ins = pe.matmul(ps_w[:, qk], w_qkv[:, n, wx, c, j * P:(j + 1) * P], xp[xx][:, c],
                                            start=(k == 0), stop=(k == 3 * C - 1))
                            k += 1
                    return ins

                def tokens_major(out, left, right, chunks, tiles=range(NT), products=PRODUCTS):
                    for t in tiles:
                        k = 0
                        for c in range(chunks):
                            for rx, lx in products:
                                ins = pe.matmul(out[:, t // 2, (t % 2) * D:(t % 2 + 1) * D], left[lx][:, c, t * P:(t + 1) * P],
                                                right(rx, c), start=(k == 0), stop=(k == len(products) * chunks - 1))
                                k += 1
                    return ins

                for s in steps:
                    k = s[0]
                    if k in ("T", "MS", "V", "OP"):
                        take_w(s, 0, 1)
                    if first:
                        if k in ("QK", "PP"):
                            pe.wait_ge(wlo_ready, {"QK": 2, "PP": 4}[k])
                        elif k == "V":
                            pe.wait_ge(wlo_ready, 6)
                        elif k == "FG":
                            pe.wait_ge(flo_ready, 2 * C * (s[1] // (NH // 2) + 1))
                        elif k == "DN":
                            pe.wait_ge(flo_ready, 4 * C + NH)
                        elif k == "MS":
                            pe.wait_ge(same_ready, 2)
                        elif k == "M":
                            pe.wait_ge(masks_ready, 6)
                    if k == "WT":
                        n = s[1]
                        take_s(s, n % 2)
                        pe.wait_ge(converted[n // C % 2 if n < 4 * C else 2], 1)
                        for m, src in enumerate(turned_parts(n)[2]):
                            ins = pe.transpose(ps_s[:, n % 2, m * P:(m + 1) * P], src, ident[:])
                        ins.then_inc(turned, 1)
                    elif k == "T":
                        pe.wait_ge(ln_done, now(ln_done, i, NT))
                        for c in range(C):
                            for t in range(NT):
                                ins = pe.transpose(ps_w[:, c, t * P:(t + 1) * P], xn[:, t, c * P:(c + 1) * P], ident[:])
                        ins.then_inc(xt_ready, 1)
                    elif k == "QK":
                        j = s[1]
                        pe.wait_ge(xlo_ready, now(xlo_ready, i, 1))
                        for z in range(2):
                            take_w(s, z)
                            project(z, j, z).then_inc(qk_ready, 1)
                    elif k == "PP":
                        j = s[1]
                        for z in range(2):
                            take_w(s, z)
                            project(2 + z, j, z).then_inc(pp_ready, 1)
                    elif k == "MS":
                        j = s[1]
                        pe.wait_ge(sq_ready, now(sq_ready, i, j + 1))
                        for z in range(2):
                            ins = pe.matmul(ps_w[:, z], same_head[:], feat_w[:, z], start=True, stop=True)
                        ins.then_inc(ms_ready, 1)
                    elif k == "V":
                        tokens_major(ps_w, xp, lambda r, c: w_qkv[:, 4, r, c], C).then_inc(v_ready, 1)
                    elif k == "FG":
                        n = s[1]
                        for g in range(2):
                            if n % 2:
                                take_s(s, g)
                            else:
                                take_w(s, g)
                            k2 = 0
                            for c in range(C):
                                for wx, xx in ffn_products:
                                    ins = pe.matmul(hidden(n)[:, g], w_gu[:, g, wx, c, n * P:(n + 1) * P], xp[xx][:, c],
                                                    start=(k2 == 0), stop=(k2 == len(ffn_products) * C - 1))
                                    k2 += 1
                            ins.then_inc((gate_ready, up_ready)[g], 1)
                    elif k == "DN":
                        t = s[1]
                        pe.wait_ge(hlo_ready, now(hlo_ready, i, NH))
                        if t % 2 == 0:
                            take_w(s, t // 2)
                        tokens_major(ps_w, hp, lambda r, c: w_d[:, r, c], NH, [t], ffn_products).then_inc(down_ready, 1)
                    elif k == "AT":
                        c = s[1]
                        pe.wait_ge(o_normed, now(o_normed, i, 2 * c + 2))
                        take_w(s, c)
                        for t in range(NT):
                            ins = pe.transpose(ps_w[:, c, t * P:(t + 1) * P], attn[:, t, c * P:(c + 1) * P], ident[:])
                        ins.then_inc(at_ready, 1)
                    elif k == "OP":
                        pe.wait_ge(aolo_ready, now(aolo_ready, i, C))
                        tokens_major(ps_w, aop, lambda r, c: w_o[:, r, c], C).then_inc(op_ready, 1)
                    elif k == "M":
                        _, j, q, f = s
                        n = q * FILLS + f
                        if f == 0:
                            if j == 0:
                                pe.wait_ge(doubled, now(doubled, i, 32))
                            else:
                                pe.wait_ge(doubled, past(doubled, i, 64))
                        if n >= 2:
                            pe.wait_ge(max_read[j], now(max_read[j], i, n - 1))
                        elif j == 0:
                            pe.wait_ge(max_read[1], now(max_read[1], i, 2 * FILLS - 1 + n))
                        else:
                            pe.wait_ge(max_read[0], past(max_read[0], i, 2 * FILLS - 1 + n))
                        for h2, qt, col, width in M_FILL[f % 5]:
                            head = QH * q + 2 * (f // 5) + h2
                            o = ps_m[:, f % 2, col:col + width]
                            pe.matmul(o, stacks[0:2 * R, j, head, Q, qt * P:(qt + 1) * P], stacks[0:2 * R, j, head, KH, 0:width],
                                      start=True, stop=False)
                            ins = pe.matmul(ps_m[:, f % 2, col + width - P:col + width], big_ident[:], mask_m[:], start=False, stop=True)
                        ins.then_inc(max_filled[j], 1)
                    elif k == "LK":
                        pe.wait_ge(low_summed, 3)
                        take_t(i, s, steps, first)
                        pe.transpose(ps_t[0:1, 0:P], low[:, 2 * C + NH:2 * C + NH + 1], ident[:]).then_inc(low_turned, 1)
                    elif k == "ST":
                        _, j, q = s
                        pe.wait_ge(neg_ready[j], now(neg_ready[j], i, q + 1))
                        take_t(i, s, steps, first)
                        for t in range(NT):
                            ins = pe.matmul(ps_t[0:QH, t * P:(t + 1) * P], neg_shift[:, q, t], big_ident[:], start=True, stop=True)
                        ins.then_inc(turned_max[j], 1)
                    elif k == "S":
                        _, w, q, f = s
                        n = (2 * w + q) * FILLS + f
                        if f == 0:
                            if w == 0:
                                if not first:
                                    pe.wait_ge(shift_stored[0][q], past(shift_stored[0][q], i, 16))
                            else:
                                pe.wait_ge(shift_stored[1][q], now(shift_stored[1][q], i, 16))
                        take_s(s, f % 2)
                        for h2, kt, col, width in S_FILL[f % 5]:
                            head = QH * q + 2 * (f // 5) + h2
                            o = ps_s[:, f % 2, col:col + width]
                            keys, queries = slice(kt * P, (kt + 1) * P), slice(kt * P, S)
                            pe.matmul(o, stacks[0:2 * R + 1, w, head, KH, keys], stacks[0:2 * R + 1, w, head, Q, queries], start=True, stop=False)
                            pe.matmul(o, stacks[0:2 * R, w, head, KL, keys], stacks[0:2 * R, w, head, Q, queries], start=False, stop=False)
                            ins = pe.matmul(ps_s[:, f % 2, col:col + P], big_ident[:], mask_t[:], start=False, stop=True)
                        ins.then_inc(s_filled, 1)
                    elif k == "PV":
                        qd = s[1]
                        pe.wait_ge(exp_done, now(exp_done, i, FILLS * (qd + 1)))
                        pe.wait_ge(o_copied, now(o_copied, i, qd))
                        if qd == 0:
                            if not first:
                                pe.wait_ge(v_stored, past(v_stored, i, 1))
                        for kt in range(NT):
                            for c in range(QH):
                                c0 = p_columns(c, kt)
                                ins = pe.matmul(ps_o[32 * c:32 * c + HD + 1, kt * P:S], v_sb[:, kt, QH * qd + c, :],
                                                probs[:, qd % 2, c0:c0 + S - kt * P], start=(kt == 0), stop=(kt == NT - 1))
                        ins.then_inc(pv_done, 1)
                    elif k == "OT":
                        q = s[1]
                        pe.wait_ge(o_copied, now(o_copied, i, q + 1))
                        take_t(i, s, steps, first)
                        for t in range(NT):
                            ins = pe.transpose(ps_t[:, t * P:(t + 1) * P], o_sb[:, t * P:(t + 1) * P], ident[:])
                        ins.then_inc(o_turned, 1)

            def take_t(i, s, steps, first):
                users = [u for u in steps if u[0] in ("ST", "OT", "LK")]
                at = users.index(s)
                if at:
                    u = users[at - 1]
                    if u[0] == "LK":
                        pe.wait_ge(low_known, 1)
                    elif u[0] == "ST":
                        pe.wait_ge(shift_ready[u[1]], now(shift_ready[u[1]], i, u[2] + 1))
                    else:
                        pe.wait_ge(o_normed, now(o_normed, i, u[1] + 1))
                else:
                    if not first:
                        pe.wait_ge(shift_ready[0], past(shift_ready[0], i, 2))
                    if not first:
                        pe.wait_ge(o_normed, past(o_normed, i, 4))

            emit(0, pieces(FIRST), first=True)
            pe.wait_ge(cleared, 2)
            with pe.register("any_low") as any_low:
                pe.wait_ge(low_known, 1)
                pe.reg_load(any_low, low_seen[0:1, 0:1])
                with pe.If_ne(any_low, 0):
                    with pe.Fori(1, B) as i:
                        emit(i, pieces(LOOP))
                    emit(B, pieces(LAST))
                with pe.Else():
                    with pe.Fori(1, B) as i:
                        emit(i, pieces(LOOP), whole=False)
                    emit(B, pieces(LAST), whole=False)


_INS = ['L0_attn_x', 'L0_attn_Wq', 'L0_attn_Wk', 'L0_attn_Wv', 'L0_attn_Wo', 'L0_attn_Wqp', 'L0_attn_Wkp',
        'L0_attn_lambda_raw', 'L0_ffn_w_gate', 'L0_ffn_w_up', 'L0_ffn_w_down']


def kernel(**inputs):
    import numpy as _np
    import concourse.bacc as _bacc
    from concourse import mybir as _mybir
    from concourse.bass_utils import run_bass_kernel_spmd as _run

    nc = _bacc.Bacc("TRN2", target_bir_lowering=False, num_devices=1)
    arrays, args = {}, []
    for name in _INS:
        a = _np.ascontiguousarray(inputs[name])
        arrays[f"in_{name}"] = a
        args.append(nc.dram_tensor(f"in_{name}", a.shape, _mybir.dt.from_np(a.dtype), kind="ExternalInput").ap())
    shape = inputs['L0_attn_x'].shape
    out = nc.dram_tensor("out_0", shape, _mybir.dt.float32, kind="ExternalOutput").ap()
    phase_attention_and_ffn(nc, *args, out)
    r = _run(nc, [arrays], core_ids=[0])
    return r.results[0]["out_0"]
```
